# Optimizing a Trainium2 kernel written in Bass

```python
import numpy as np
import jax
import jax.numpy as jnp

def _softmax(x, axis=-1):
    return jax.nn.softmax(x, axis=axis)

def _gelu(x):
    return jax.nn.gelu(x, approximate=True)

def _silu(x):
    return jax.nn.silu(x)

def _sigmoid(x):
    return jax.nn.sigmoid(x)

def _layernorm(x, axis=-1, eps=1e-05):
    m = jnp.mean(x, axis=axis, keepdims=True)
    v = jnp.var(x, axis=axis, keepdims=True)
    return (x - m) / jnp.sqrt(v + eps)

def _scatter_add(tgt, idx, src, axis=0):
    return tgt.at[idx].add(src)

def _segment_sum(src, seg, n):
    return jax.ops.segment_sum(src, seg, n)
kernel_name = 'mk_adj_preln_d4_adj_r2_58a23c'

def setup_inputs(seed: int=0):
    np.random.seed(seed)
    _w = jnp.asarray

    def _rec_inputs():
        import jax
        import jax.numpy as jnp
        _gk = jax.random.key(seed)
        x = -0.000929 + 1 * jax.random.normal(jax.random.fold_in(_gk, 1), (8, 2048, 64), jnp.float32)
        _a = jax.random.bernoulli(jax.random.fold_in(_gk, 2), 0.000976562, (2048, 2048))
        _a = jnp.logical_or(_a, jnp.swapaxes(_a, -1, -2))
        _a = jnp.logical_or(_a, jnp.eye(2048, dtype=bool))
        adj = _a.astype(jnp.int32)
        return (x, adj)
    x, adj = _rec_inputs()

    def _L0_gnn_setup():
        import jax, jax.numpy as jnp
        import numpy as np
        ALPHA = 0.2
        BN_EPS = 1e-05
        NEG_INF = -9000000000000000.0
        key = jax.random.key(seed)
        k1, k2, k3, k4 = jax.random.split(key, 4)
        B, N, Fin, Fout = (4, 2048, 64, 64)
        h = jax.random.normal(k1, (B, N, Fin), dtype=jnp.float32)
        adj = jax.random.randint(k2, (N, N), 0, 2, dtype=jnp.int32)
        gain = 1.414
        bW = gain * np.sqrt(6.0 / (Fin + Fout))
        W = jax.random.uniform(k3, (Fin, Fout), dtype=jnp.float32, minval=-bW, maxval=bW)
        ba = gain * np.sqrt(6.0 / (2 * Fout + 1))
        a = jax.random.uniform(k4, (2 * Fout, 1), dtype=jnp.float32, minval=-ba, maxval=ba)
        gamma = jnp.ones((N,), dtype=jnp.float32)
        beta = jnp.zeros((N,), dtype=jnp.float32)
        return {'h': h, 'adj': adj, 'W': W, 'a': a, 'gamma': gamma, 'beta': beta}
    _L0_gnn_all = _L0_gnn_setup()
    _L0_gnn_in = {k: v for k, v in _L0_gnn_all.items() if k in ('W', 'a', 'gamma', 'beta')}
    del _L0_gnn_all

    def _L1_gnn_setup():
        import jax, jax.numpy as jnp
        import numpy as np
        NEG = -1e+16
        LN_EPS = 1e-05

        def _gat_layer(h, mask, b):
            scores = jnp.einsum('...nd,...md->...nm', h, h)
            scores = jnp.where(mask, scores, NEG)
            attn = jax.nn.softmax(scores, axis=-1)
            return jnp.einsum('...nm,...md->...nd', attn, h) + b
        key = jax.random.key(seed)
        ks = jax.random.split(key, 6)
        B, N, C, H, D = (8, 1024, 64, 4, 64)
        x = jax.random.normal(ks[0], (B, N, C), dtype=jnp.float32)
        graph = jax.random.randint(ks[1], (N, N), 0, 2, dtype=jnp.int32)
        bnd_h = float(np.sqrt(6.0 / (C + D)))
        Wh = jax.random.uniform(ks[2], (H, D, C), jnp.float32, -bnd_h, bnd_h)
        bh = jnp.zeros((H, D), jnp.float32)
        bnd_o = float(np.sqrt(6.0 / (H * D + D)))
        Wo = jax.random.uniform(ks[3], (D, H * D), jnp.float32, -bnd_o, bnd_o)
        bo = jnp.zeros((D,), jnp.float32)
        gamma = jnp.ones((D,), jnp.float32)
        beta = jnp.zeros((D,), jnp.float32)
        return {'x': x, 'graph': graph, 'Wh': Wh, 'bh': bh, 'Wo': Wo, 'bo': bo, 'gamma': gamma, 'beta': beta}
    _L1_gnn_all = _L1_gnn_setup()
    _L1_gnn_in = {k: v for k, v in _L1_gnn_all.items() if k in ('Wh', 'bh', 'Wo', 'bo', 'gamma', 'beta')}
    del _L1_gnn_all

    def _L2_gnn_setup():
        import jax, jax.numpy as jnp
        import numpy as np
        B, N, C_IN, C_OUT = (8, 2048, 64, 64)
        NEG_INF = -9000000000000000.0
        LEAKY_SLOPE = 0.01
        key = jax.random.key(seed)
        kx, ka, kw, kq, kk = jax.random.split(key, 5)
        X = jax.random.normal(kx, (B, N, C_IN), dtype=jnp.float32)
        A = jax.random.randint(ka, (N, N), 0, 2, dtype=jnp.int32)

        def xavier(k, shape):
            fan_in, fan_out = shape
            bound = 1.414 * np.sqrt(6.0 / (fan_in + fan_out))
            return jax.random.uniform(k, shape, jnp.float32, -bound, bound)
        weight = xavier(kw, (C_IN, C_OUT))
        query = xavier(kq, (C_IN, C_OUT))
        key_p = xavier(kk, (C_IN, C_OUT))
        return {'X': X, 'A': A, 'weight': weight, 'query': query, 'key_p': key_p}
    _L2_gnn_all = _L2_gnn_setup()
    _L2_gnn_in = {k: v for k, v in _L2_gnn_all.items() if k in ('weight', 'query', 'key_p')}
    del _L2_gnn_all

    def _L3_gnn_setup():
        import jax, jax.numpy as jnp
        import numpy as np
        ALPHA = 0.2
        MASK_VAL = -9000000000000000.0
        B, N, FIN, FOUT = (8, 1024, 64, 64)
        key = jax.random.key(seed)
        k1, k2, k3, k4 = jax.random.split(key, 4)
        x = jax.random.normal(k1, (B, N, FIN), dtype=jnp.float32)
        adj = jax.random.randint(k2, (N, N), 0, 2, dtype=jnp.int32)
        W = jax.random.normal(k3, (FOUT, FIN), dtype=jnp.float32) * 0.1
        a = jax.random.normal(k4, (2 * FOUT, 1), dtype=jnp.float32) * 0.1
        return {'x': x, 'adj': adj, 'W': W, 'a': a}
    _L3_gnn_all = _L3_gnn_setup()
    _L3_gnn_in = {k: v for k, v in _L3_gnn_all.items() if k in ('W', 'a')}
    del _L3_gnn_all
    return {'x': x, 'adj': adj, 'L0_gnn_W': _L0_gnn_in['W'], 'L0_gnn_a': _L0_gnn_in['a'], 'L0_gnn_gamma': _L0_gnn_in['gamma'], 'L0_gnn_beta': _L0_gnn_in['beta'], 'L1_gnn_Wh': _L1_gnn_in['Wh'], 'L1_gnn_bh': _L1_gnn_in['bh'], 'L1_gnn_Wo': _L1_gnn_in['Wo'], 'L1_gnn_bo': _L1_gnn_in['bo'], 'L1_gnn_gamma': _L1_gnn_in['gamma'], 'L1_gnn_beta': _L1_gnn_in['beta'], 'L2_gnn_weight': _L2_gnn_in['weight'], 'L2_gnn_query': _L2_gnn_in['query'], 'L2_gnn_key_p': _L2_gnn_in['key_p'], 'L3_gnn_W': _L3_gnn_in['W'], 'L3_gnn_a': _L3_gnn_in['a']}

def reference(x, adj, L0_gnn_W, L0_gnn_a, L0_gnn_gamma, L0_gnn_beta, L1_gnn_Wh, L1_gnn_bh, L1_gnn_Wo, L1_gnn_bo, L1_gnn_gamma, L1_gnn_beta, L2_gnn_weight, L2_gnn_query, L2_gnn_key_p, L3_gnn_W, L3_gnn_a):
    import jax
    import jax.numpy as jnp

    def _L0_gnn_ref(h, adj, W, a, gamma, beta):
        import jax, jax.numpy as jnp
        import numpy as np
        ALPHA = 0.2
        BN_EPS = 1e-05
        NEG_INF = -9000000000000000.0
        N = adj.shape[0]
        Fout = W.shape[1]
        dk = jnp.asarray(N, h.dtype) ** 0.5
        Wh = jnp.einsum('bnf,fo->bno', h, W)
        Wh1 = Wh @ a[:Fout]
        Wh2 = Wh @ a[Fout:]
        e = (Wh1 + jnp.swapaxes(Wh2, 1, 2)) / dk
        e = jax.nn.leaky_relu(e, negative_slope=ALPHA)
        scores = jnp.where(adj[None] > 0, e, NEG_INF)
        attention = jax.nn.softmax(scores, axis=2)
        h_prime = jnp.einsum('bij,bjo->bio', attention, Wh)
        mean = h_prime.mean(axis=(0, 2), keepdims=True)
        var = h_prime.var(axis=(0, 2), keepdims=True)
        h_prime = gamma[None, :, None] * (h_prime - mean) * jax.lax.rsqrt(var + BN_EPS) + beta[None, :, None]
        out = h_prime + h
        return jax.nn.elu(out)

    def _L1_gnn_ref(x, graph, Wh, bh, Wo, bo, gamma, beta):
        import jax, jax.numpy as jnp
        import numpy as np
        NEG = -1e+16
        LN_EPS = 1e-05

        def _gat_layer(h, mask, b):
            scores = jnp.einsum('...nd,...md->...nm', h, h)
            scores = jnp.where(mask, scores, NEG)
            attn = jax.nn.softmax(scores, axis=-1)
            return jnp.einsum('...nm,...md->...nd', attn, h) + b
        B, N, C = x.shape
        H, D, _ = Wh.shape
        mask = graph + jnp.eye(N, dtype=graph.dtype) > 0
        h = jnp.einsum('bnc,hdc->bhnd', x, Wh)
        out_h = _gat_layer(h, mask[None, None], bh[None, :, None, :])
        cat = jnp.transpose(out_h, (0, 2, 1, 3)).reshape(B, N, H * D)
        z = jax.nn.leaky_relu(cat, negative_slope=0.2)
        h2 = jnp.einsum('bnk,dk->bnd', z, Wo)
        out2 = _gat_layer(h2, mask[None], bo)
        z2 = jax.nn.leaky_relu(out2, negative_slope=0.2)
        mu = jnp.mean(z2, axis=-1, keepdims=True)
        var = jnp.mean(jnp.square(z2 - mu), axis=-1, keepdims=True)
        out = (z2 - mu) * jax.lax.rsqrt(var + LN_EPS) * gamma + beta
        return out

    def _L2_gnn_ref(X, A, weight, query, key_p):
        import jax, jax.numpy as jnp
        import numpy as np
        B, N, C_IN, C_OUT = (8, 2048, 64, 64)
        NEG_INF = -9000000000000000.0
        LEAKY_SLOPE = 0.01
        n = X.shape[1]
        idx = jnp.arange(n)
        adj = A.at[idx, idx].set(1)
        out = jnp.einsum('bni,io->bno', X, weight)
        q = jnp.einsum('bni,io->bno', X, query)
        k = jnp.einsum('bni,io->bno', X, key_p)
        att = jnp.einsum('bnd,bmd->bnm', q, k)
        att = jax.nn.leaky_relu(att, LEAKY_SLOPE)
        att = jnp.where(adj[None, :, :] > 0, att, NEG_INF)
        att = jax.nn.softmax(att, axis=-1)
        return jnp.einsum('bnm,bmo->bno', att, out)

    def _L3_gnn_ref(x, adj, W, a):
        import jax, jax.numpy as jnp
        import numpy as np
        ALPHA = 0.2
        MASK_VAL = -9000000000000000.0
        B, N, FIN, FOUT = (8, 1024, 64, 64)
        h = jnp.einsum('bnf,of->bno', x, W)
        f_out = h.shape[-1]
        a1 = a[:f_out, 0]
        a2 = a[f_out:, 0]
        e_i = h @ a1
        e_j = h @ a2
        e = jax.nn.leaky_relu(e_i[:, :, None] + e_j[:, None, :], negative_slope=ALPHA)
        e = jnp.where(adj[None, :, :] > 0, e, MASK_VAL)
        attention = jax.nn.softmax(e, axis=2)
        h_prime = jnp.einsum('bij,bjo->bio', attention, h)
        return jax.nn.relu(h_prime)
    h = jnp.maximum(_layernorm(x, axis=-1), 0.0)
    x = x + _L0_gnn_ref(h, adj, L0_gnn_W, L0_gnn_a, L0_gnn_gamma, L0_gnn_beta)
    h = jnp.maximum(_layernorm(x, axis=-1), 0.0)
    x = x + _L1_gnn_ref(h, adj, L1_gnn_Wh, L1_gnn_bh, L1_gnn_Wo, L1_gnn_bo, L1_gnn_gamma, L1_gnn_beta)
    h = jnp.maximum(_layernorm(x, axis=-1), 0.0)
    x = x + _L2_gnn_ref(h, adj, L2_gnn_weight, L2_gnn_query, L2_gnn_key_p)
    h = jnp.maximum(_layernorm(x, axis=-1), 0.0)
    x = x + _L3_gnn_ref(h, adj, L3_gnn_W, L3_gnn_a)
    return x

_drawn_inputs = setup_inputs


def setup_inputs(seed=0):
    import zlib

    import numpy as np

    out = dict(_drawn_inputs(seed))
    spreads = {'L0_gnn_gamma': (1.0, 0.2),
     'L0_gnn_beta': (0.0, 0.1),
     'L1_gnn_bh': (0.0, 0.1),
     'L1_gnn_bo': (0.0, 0.1),
     'L1_gnn_gamma': (1.0, 0.2),
     'L1_gnn_beta': (0.0, 0.1)}
    factors = {'L0_gnn_a': 8.0, 'L3_gnn_a': 4.889}
    for name, (base, spread) in spreads.items():
        noise = np.random.default_rng([zlib.crc32(name.encode()), seed]).standard_normal(out[name].shape)
        drawn = base * np.exp(spread * noise) if base else spread * noise
        out[name] = jnp.asarray(drawn.astype(out[name].dtype))
    for name, factor in factors.items():
        out[name] = (out[name] * factor).astype(out[name].dtype)
    return out
```

```python
import concourse.bass as bass
from concourse import mybir
from contextlib import ExitStack

F32 = mybir.dt.float32
BF16 = mybir.dt.bfloat16
I32 = mybir.dt.int32
ALU = mybir.AluOpType
ACT = mybir.ActivationFunctionType
AX = mybir.AxisListType

P = 128
B, N, D = 8, 2048, 64
NT = N // P
E = B * D
HEADS = 4
EPS = 1e-5
NEG = -9e15
DK = float(N) ** 0.5

SLOTS = [15, 8, 7, 7, 6, 6, 6, 5, 5, 5, 4, 4, 4, 3, 3, 2]
NL = 16
RW = D + 2
XS = E + 2 + 2 * NL + 1

UNITS = ([dict(layer=0, keys=0, values=0, own=0, w=RW, slope=0.2, factor=1.0 / DK, add=True)]
         + [dict(layer=1, keys=1 + h, values=1 + h, own=1 + h, w=D, slope=None, factor=1.0, add=False)
            for h in range(HEADS)]
         + [dict(layer=1, keys=5, values=5, own=None, w=D, slope=None, factor=1.0, add=False)]
         + [dict(layer=2, keys=6, values=7, own=8, w=D, slope=0.01, factor=1.0, add=False)]
         + [dict(layer=3, keys=9, values=9, own=9, w=RW, slope=0.2, factor=1.0, add=True)])
NTAB = 10
TABW = [RW] + [D] * 8 + [RW]
PROJ = [([0], RW), ([1, 2, 3, 4], D), ([6, 7, 8], D), ([9], RW)]
BRANCHES = [[0], [1, 2, 3, 4, 5], [6], [7]]

ROWBUF = [SLOTS[0] * RW * B, SLOTS[0] * E, SLOTS[1] * E, SLOTS[1] * E]
NRB = len(ROWBUF)
CHUNK = 7
NOWN = 3
NOT = 3


def gather_batches():
    out = []
    for u, un in enumerate(UNITS):
        for t in range(NT):
            for tab in dict.fromkeys([un["keys"], un["values"]]):
                out.append((u, t, tab, SLOTS[t]))
    return out


BATCHES = gather_batches()
BATCH_OF = {(u, t, tab): g for g, (u, t, tab, _) in enumerate(BATCHES)}


def gathered_by(g):
    return 16 * sum(BATCHES[i][3] for i in range(g % NRB, g + 1, NRB))


OWNS = [(u, t) for u, un in enumerate(UNITS) for t in range(NT) if un["own"] is not None]
OWN_OF = {ut: o for o, ut in enumerate(OWNS)}


def stored_by(layer, parity):
    return 16 * (NT // 2) * sum(len(PROJ[l][0]) for l in range(layer + 1))


def program(nc, x, adj, L0_W, L0_a, L0_gamma, L0_beta, L1_Wh, L1_bh, L1_Wo, L1_bo, L1_gamma, L1_beta,
            L2_weight, L2_query, L2_key, L3_W, L3_a, out):
    xs = nc.dram_tensor("xs", (N, XS), F32, kind="Internal").ap()
    keyd = nc.dram_tensor("keyd", (N,), F32, kind="Internal").ap()
    rankd = nc.dram_tensor("rankd", (N,), F32, kind="Internal").ap()
    tabs = [nc.dram_tensor(f"tab{i}", (N, B * TABW[i]), F32, kind="Internal").ap() for i in range(NTAB)]
    out_rows = out.rearrange("b n d -> (b n) d")

    ctx = ExitStack()
    with ctx:
        def sb(name, shape, dt=F32):
            return ctx.enter_context(nc.sbuf_tensor(name, shape, dt))

        def ps(name, shape, dt=F32):
            return ctx.enter_context(nc.psum_tensor(name, shape, dt))

        def sem(name):
            return ctx.enter_context(nc.semaphore(name))

        XH = sb("XH", [P, 2 * NT * E])
        X = XH[:, 0:NT * E].rearrange("p (t e) -> p t e", t=NT)
        H = XH[:, NT * E:].rearrange("p (t e) -> p t e", t=NT)
        mask = XH[:, :].bitcast(BF16).rearrange("p (t n) -> p t n", t=NT)[:, :, :]
        arena_w = sum(ROWBUF) + CHUNK * E
        arena = sb("arena", [P, arena_w])
        rowbuf = [arena[:, sum(ROWBUF[:i]):sum(ROWBUF[:i + 1])] for i in range(NRB)]
        prod = arena[:, sum(ROWBUF):sum(ROWBUF) + CHUNK * E]
        stage = arena[:, 0:2 * 4 * E].rearrange("p (s e) -> p s e", s=2)
        sq = arena[:, 8 * E:16 * E].rearrange("p (s e) -> p s e", s=2)
        XR = arena[:, 0:NT * XS].rearrange("p (t e) -> p t e", t=NT)
        at = NT * XS
        adjt = arena[:, at:at + 3 * N].bitcast(I32).rearrange("p (s n) -> p s n", s=3)
        at += 3 * N
        brow = arena[:, at:at + N]
        at += N
        ranked = arena[:, at:at + N]
        at += N
        junk = arena[:, at:at + N]
        assert at + N <= arena_w

        def take(width, at=[0]):
            at[0] += width
            assert at[0] <= arena_w
            return arena[:, at[0] - width:at[0]]

        far_out = take(NT * E).rearrange("p (t e) -> p t e", t=NT)
        far_rows = [take(NT * RW) for _ in range(3)]
        far_pairs = [take(NT * 2).rearrange("p (t c) -> p t c", c=2) for _ in range(2)]
        far_kT, far_qT, far_e, far_pT, far_bias = (take(N) for _ in range(5))
        far_adj = take(N).bitcast(I32)
        far_q = take(P)
        own = sb("own", [P, NOWN, RW * B])
        ot = sb("ot", [P, NOT, E])
        aux = sb("aux", [P, 2, E])
        hT = sb("hT", [P, 2, E])
        ident = sb("ident", [P, P])
        other = sb("other", [P, P])
        WB = [sb("WB0", [P, 1, 2, RW]), sb("WB1", [P, HEADS, 2, D]), sb("WB2", [P, 3, 2, D]),
              sb("WB3", [P, 1, 2, RW])]
        WoB = sb("WoB", [P, HEADS, 2, D])
        wload = ot[:, :, :].rearrange("p s e -> p (s e)")
        ones = own[:, 0, 0:P]
        abc = own[:, 1, 0:4 * D].rearrange("p (l o) -> p l o", l=2)
        wtmp = own[:, 2, 0:D]
        turned = aux[:, 1, 64:64 + 3 * P].rearrange("p (i c) -> p i c", i=3)
        bh = sb("bh", [P, HEADS])
        rows64 = sb("rows64", [P, 3, D])
        SI = sb("SI", [P, NT, XS - E])
        sc = sb("sc", [P, 2, SLOTS[0] * B])
        sc2 = sb("sc2", [P, SLOTS[0] * B])
        mx = sb("mx", [P, 2, B])
        stats = sb("stats", [P, 4, NT * B])
        sd = sb("sd", [P, NT * B])
        bn = sb("bn", [P, 2, 16])
        ln = sb("ln", [P, 4, 4 * B])
        epsc = sb("epsc", [P, 1])
        far_sum = sb("far_sum", [P, 3])
        small = sb("small", [P, 16, NT])
        flag = sb("flag", [P, 1], I32)
        ranki = sb("ranki", [P, NT], I32)
        iot = sb("iot", [P, NT], I32)
        lists = aux[:, 0, 0:NT * NL].rearrange("p (t k) -> p t k", t=NT)
        valid = aux[:, 0, NT * NL:2 * NT * NL].rearrange("p (t k) -> p t k", t=NT)
        cand = aux[:, 1, 0:64].rearrange("p (i c) -> p i c", i=2)

        gbias = SI[:, :, 2 + NL:2 + 2 * NL]
        gidx = SI[:, :, 2:2 + NL].bitcast(I32)
        gamma = SI[:, :, 0:1]
        beta = SI[:, :, 1:2]
        node = SI[:, :, 2 + 2 * NL:].bitcast(I32)

        tps = [ps(f"tps{i}", [P, 512]) for i in range(2)]
        pps = [ps(f"pps{i}", [P, 512]) for i in range(4)]
        wps = [ps(f"wps{i}", [P, 512]) for i in range(2)]

        adj_loaded = [sem(f"adj_loaded{i}") for i in range(3)]
        adj_used = sem("adj_used")
        x_in = sem("x_in")
        w_in = sem("w_in")
        iota_made = sem("iota_made")
        ident_made = sem("ident_made")
        key_made = sem("key_made")
        key_stored = sem("key_stored")
        key_rows = sem("key_rows")
        rank_made = sem("rank_made")
        rank_stored = sem("rank_stored")
        rank_rows = sem("rank_rows")
        bad_made = sem("bad_made")
        bad_summed = sem("bad_summed")
        flag_made = sem("flag_made")
        ordered = sem("ordered")
        scattered = sem("scattered")
        x_loaded = sem("x_loaded")
        w_turned = sem("w_turned")
        w_built = sem("w_built")
        centred = sem("centred")
        squared = sem("squared")
        squares_used = sem("squares_used")
        var_made = sem("var_made")
        sd_made = sem("sd_made")
        h_made = sem("h_made")
        h_turned = sem("h_turned")
        hT_made = sem("hT_made")
        projected = sem("projected")
        staged = sem("staged")
        stage_stored = [sem(f"stage_stored{i}") for i in range(2)]
        h2_stored = sem("h2_stored")
        gathered = [sem(f"gathered{i}") for i in range(NRB)]
        rows_used = [sem(f"rows_used{i}") for i in range(NRB)]
        own_loaded = [sem(f"own_loaded{i}") for i in range(NOWN)]
        own_used = sem("own_used")
        scored = sem("scored")
        exped = sem("exped")
        attended = sem("attended")
        bn_made = sem("bn_made")
        bn_rooted = sem("bn_rooted")
        elu_in = sem("elu_in")
        elu_exped = sem("elu_exped")
        z_turned = sem("z_turned")
        zT_made = sem("zT_made")
        zT_leaky = sem("zT_leaky")
        wo_made = sem("wo_made")
        wo_used = sem("wo_used")
        z_centred = sem("z_centred")
        z_squared = sem("z_squared")
        z_var = sem("z_var")
        z_rooted = sem("z_rooted")
        far_loaded = sem("far_loaded")
        far_adj_loaded = sem("far_adj_loaded")
        far_source = sem("far_source")
        far_turned = sem("far_turned")
        far_kT_made = sem("far_kT_made")
        far_q_made = sem("far_q_made")
        far_bias_made = sem("far_bias_made")
        far_scored = sem("far_scored")
        far_masked = sem("far_masked")
        far_exped = sem("far_exped")
        far_p_turned = sem("far_p_turned")
        far_pT_made = sem("far_pT_made")
        far_summed = sem("far_summed")
        dve_done_far = [sem(f"dve_done_far{u}") for u in range(len(UNITS))]
        x_final = sem("x_final")
        out_stored = sem("out_stored")
        dve_done = {k: sem(f"dve_done_{k}") for k in
                    ["order", "prep0", "prep1", "prep2", "prep3", "near0", "near1", "near2", "near3",
                     "end0", "end1", "end2", "end3"]}

        block = ctx.enter_context(nc.Block())

        ADJ = adj.rearrange("(t p) n -> p t n", p=P)

        def store_h2(sp, t):
            sp.wait_ge(wo_used, NT * (HEADS - 1) + t + 1)
            sp.dma_start(tabs[5][t * P:(t + 1) * P, :], H[:, t, :]).then_inc(h2_stored, 16)

        def load_far(sp, u):
            un = UNITS[u]
            w = un["w"]
            queries = un["keys"] if un["own"] is None else un["own"]
            with sp.Fori(0, B) as b:
                sp.wait_ge(far_summed, NT * (B * u + b) + 1)
                for to, tab in zip(far_rows, (un["keys"], un["values"], queries)):
                    rows = tabs[tab].rearrange("(t p) (b c) -> p t b c", p=P, b=B)
                    sp.dma_start(to[:, 0:NT * w].rearrange("p (t c) -> p t c", t=NT).unsqueeze(2),
                                 rows[:, :, bass.ds(b, 1), :]).then_inc(far_loaded, 16)
                with sp.Fori(0, NT) as t:
                    sp.wait_ge(far_bias_made, NT * (B * u + b) + t + 1)
                    sp.dma_start(far_adj, ADJ[:, bass.ds(t, 1), :].rearrange("p o n -> p (o n)"))\
                      .then_inc(far_adj_loaded, 16)

        @block.sync
        def _(sp):
            for c in range(NT):
                if c >= 3:
                    sp.wait_ge(adj_used, c - 2)
                sp.dma_start(adjt[:, c % 3, :], ADJ[:, c, :]).then_inc(adj_loaded[c % 3], 16)
            sp.wait_ge(key_made, 1)
            sp.dma_start(keyd.rearrange("(p t) -> p t", p=P), small[:, 2, :]).then_inc(key_stored, 16)
            sp.wait_ge(key_stored, 16)
            sp.dma_start(brow, keyd.partition_broadcast(P)).then_inc(key_rows, 16)
            sp.wait_ge(rank_made, 1)
            sp.dma_start(rankd.rearrange("(p t) -> p t", p=P), small[:, 4, :]).then_inc(rank_stored, 16)
            sp.wait_ge(rank_stored, 16)
            sp.dma_start(brow, rankd.partition_broadcast(P)).then_inc(rank_rows, 16)
            sp.wait_ge(scattered, 16 * NT)
            XSV = xs.rearrange("(t p) e -> p t e", p=P)
            sp.dma_start(SI[:, :, :], XSV[:, :, E:]).then_inc(x_loaded, 16)
            for t in range(0, NT, 4):
                sp.dma_start(X[:, t:t + 4, :], XSV[:, t:t + 4, 0:E]).then_inc(x_loaded, 16)

            def load_own(u, t):
                o = OWN_OF[u, t]
                w = UNITS[u]["w"] * B
                if o >= NOWN:
                    sp.wait_ge(own_used, o - NOWN + 1)
                sp.dma_start(own[:, o % NOWN, 0:w],
                             tabs[UNITS[u]["own"]][t * P:(t + 1) * P, :]).then_inc(own_loaded[o % NOWN], 16)

            sp.wait_ge(flag_made, 1)
            far = sp.value_load(flag[0:1, 0:1], min_val=0, max_val=1)
            for layer in range(4):
                tables, w = PROJ[layer]
                for t in range(NT):
                    sp.wait_ge(staged, 4 * (NT * layer + t + 1))
                    for g, tab in enumerate(tables):
                        sp.dma_start(tabs[tab][t * P:(t + 1) * P, :],
                                     stage[:, t % 2, g * B * w:(g + 1) * B * w]).then_inc(stage_stored[t % 2], 16)
                for i in range(2):
                    sp.wait_ge(stage_stored[i], stored_by(layer, i))
                with sp.If(far == 0):
                    for u in BRANCHES[layer]:
                        if UNITS[u]["own"] is not None:
                            for t in range(NT):
                                load_own(u, t)
                                if u == HEADS and t >= 3:
                                    store_h2(sp, t - 3)
                        if u == HEADS:
                            for t in range(NT - 3, NT):
                                store_h2(sp, t)
                with sp.Else():
                    for u in BRANCHES[layer]:
                        if UNITS[u]["own"] is None:
                            sp.wait_ge(h2_stored, 16 * NT)
                        load_far(sp, u)
                        if u == HEADS:
                            for t in range(NT):
                                store_h2(sp, t)
            sp.wait_ge(out_stored, 16 * B * NT)

        @block.gpsimd
        def _(pool):
            pool.memset(ident[:, :], 0.0).then_inc(ident_made, 1)
            pool.memset(ones[:, :], 1.0).then_inc(ident_made, 1)
            pool.wait_ge(ident_made, 2)
            pool.affine_select(out=ident[:, :], in_=ident[:, :], compare_op=ALU.not_equal, fill=1.0, base=0,
                               pattern=[[-1, P]], channel_multiplier=1).then_inc(ident_made, 1)
            pool.iota(iot[:, :], pattern=[[P, NT]], base=0, channel_multiplier=1).then_inc(iota_made, 1)
            pool.wait_ge(ordered, 1)
            pool.wait_ge(x_in, 16 * NT)
            for t in range(NT):
                pool.indirect_dma_start(out=xs, out_offset=bass.IndirectOffsetOnAxis(ap=ranki[:, t:t + 1], axis=0),
                                        in_=XR[:, t, :], in_offset=None).then_inc(scattered, 16)

            def gather(u, t):
                for tab in dict.fromkeys([UNITS[u]["keys"], UNITS[u]["values"]]):
                    g = BATCH_OF[u, t, tab]
                    w = TABW[tab] * B
                    if g >= NRB:
                        pool.wait_ge(rows_used[g % NRB], g // NRB)
                    for k in range(SLOTS[t]):
                        pool.indirect_dma_start(
                            out=rowbuf[g % NRB][:, k * w:(k + 1) * w], out_offset=None, in_=tabs[tab],
                            in_offset=bass.IndirectOffsetOnAxis(ap=gidx[:, t, k:k + 1], axis=0)
                        ).then_inc(gathered[g % NRB], 16)

            def put_out(t):
                pool.wait_ge(x_final, t + 1)
                for b in range(B):
                    pool.indirect_dma_start(
                        out=out_rows, out_offset=bass.IndirectOffsetOnAxis(ap=node[:, t, :], axis=0),
                        in_=X[:, t, b * D:(b + 1) * D], in_offset=None, element_offset=b * N * D
                    ).then_inc(out_stored, 16)

            pool.wait_ge(x_loaded, 16 * 5)
            pool.wait_ge(flag_made, 1)
            far = pool.value_load(flag[0:1, 0:1], min_val=0, max_val=1)
            with pool.If(far == 0):
                for layer in range(4):
                    for i in range(2):
                        pool.wait_ge(stage_stored[i], stored_by(layer, i))
                    for u in BRANCHES[layer]:
                        if UNITS[u]["own"] is None:
                            pool.wait_ge(h2_stored, 16 * NT)
                        for t in range(NT):
                            gather(u, t)
                            if layer == 3 and t >= NRB:
                                put_out(t - NRB)
                for t in range(NT - NRB, NT):
                    put_out(t)
            with pool.Else():
                for t in range(NT):
                    put_out(t)

        @block.scalar
        def _(act):
            for t in range(NT):
                act.dma_start(XR[:, t, 0:E].rearrange("p (b d) -> p b d", b=B),
                              x[:, t * P:(t + 1) * P, :].rearrange("b n d -> n b d")).then_inc(x_in, 16)
            for i in range(2):
                for q, w in enumerate([L0_W, L2_key, L2_weight, L2_query]):
                    act.dma_start(wload[i * D:(i + 1) * D, q * D:(q + 1) * D], w).then_inc(w_in, 16)
                for hh in range(2):
                    act.dma_start(wload[:, (4 + 2 * hh + i) * D:(5 + 2 * hh + i) * D],
                                  L1_Wh.rearrange("h d c -> (h d) c")[hh * P:(hh + 1) * P, :]).then_inc(w_in, 16)
                act.dma_start(wload[0:D, 8 * D:16 * D].rearrange("p (h i d) -> p h i d", h=HEADS, i=2)[:, :, i, :],
                              L1_Wo.rearrange("o (h d) -> o h d", h=HEADS)).then_inc(w_in, 16)
                act.dma_start(wload[D:P, (8 + i) * D:(9 + i) * D], L3_W).then_inc(w_in, 16)
                act.dma_start(turned[0:HEADS, 2, i * D:(i + 1) * D], L1_bh).then_inc(w_in, 16)
            act.dma_start(turned[0:NT, 0, :], L0_gamma.rearrange("(t p) -> t p", p=P)).then_inc(w_in, 16)
            act.dma_start(turned[0:NT, 1, :], L0_beta.rearrange("(t p) -> t p", p=P)).then_inc(w_in, 16)
            act.dma_start(abc[:, 0, :], L0_a.rearrange("a o -> (a o)").partition_broadcast(P)).then_inc(w_in, 16)
            act.dma_start(abc[:, 1, :], L3_a.rearrange("a o -> (a o)").partition_broadcast(P)).then_inc(w_in, 16)
            for i, v in enumerate([L1_bo, L1_gamma, L1_beta]):
                act.dma_start(rows64[:, i, :], v.partition_broadcast(P)).then_inc(w_in, 16)

            def prep(layer):
                for g in range(4):
                    act.wait_ge(centred, 4 * layer + g + 1)
                    if g >= 2:
                        act.wait_ge(squares_used, 4 * layer + g - 1)
                    act.activation(sq[:, g % 2, :], H[:, 4 * g:4 * g + 4, :].rearrange("p t e -> p (t e)"),
                                   ACT.Square).then_inc(squared, 1)
                act.wait_ge(var_made, layer + 1)
                act.activation(sd[:, :], stats[:, 2, :], ACT.Sqrt, bias=epsc[:, 0:1], scale=1.0 / D)\
                   .then_inc(sd_made, 1)
                for t in range(NT):
                    n = NT * layer + t
                    act.wait_ge(h_turned, n + 1)
                    if n >= 2:
                        act.wait_ge(projected, 4 * (n - 1))
                    act.activation(hT[:, t % 2, :], tps[t % 2][:, :], ACT.Copy).then_inc(hT_made, 1)

            def exp(j):
                act.wait_ge(scored, j + 1)
                w = SLOTS[j % NT] * B
                act.activation(sc[:, j % 2, 0:w], sc[:, j % 2, 0:w], ACT.Exp).then_inc(exped, 1)

            def finish(u, i):
                if u == 0 and 1 <= i <= NT:
                    act.wait_ge(bn_made, i)
                    act.activation(bn[:, (i - 1) % 2, 8:9], bn[:, (i - 1) % 2, 7:8], ACT.Sqrt,
                                   bias=epsc[:, 0:1]).then_inc(bn_rooted, 1)
                if u == 0 and 2 <= i <= NT + 1:
                    t = i - 2
                    act.wait_ge(elu_in, t + 1)
                    act.activation(aux[:, t % 2, :], aux[:, t % 2, :], ACT.Exp).then_inc(elu_exped, 1)
                if 1 <= u <= HEADS and 1 <= i <= NT:
                    h, n = u - 1, NT * (u - 1) + i - 1
                    act.wait_ge(z_turned, n + 1)
                    if n >= 2:
                        act.wait_ge(wo_made, n - 1)
                    act.activation(hT[:, n % 2, :], tps[n % 2][:, :], ACT.Identity,
                                   bias=bh[:, h:h + 1]).then_inc(zT_made, 1)
                if u == 5 and 1 <= i <= NT:
                    t = i - 1
                    act.wait_ge(z_centred, t + 1)
                    act.activation(aux[:, t % 2, :], ot[:, (5 * NT + t) % NOT, :], ACT.Square).then_inc(z_squared, 1)
                if u == 5 and 2 <= i <= NT + 1:
                    t = i - 2
                    act.wait_ge(z_var, t + 1)
                    act.activation(ln[:, 3, (t % 2) * B:(t % 2 + 1) * B], ln[:, 2, (t % 2) * B:(t % 2 + 1) * B],
                                   ACT.Sqrt, bias=epsc[:, 0:1], scale=1.0 / D).then_inc(z_rooted, 1)

            def attend_far(u):
                kw = 2 if UNITS[u]["add"] else D
                with act.Fori(0, B) as b:
                    act.wait_ge(far_kT_made, B * u + b + 1)
                    with act.Fori(0, NT) as t:
                        n = NT * (B * u + b) + t
                        act.wait_ge(far_scored, n + 1)
                        act.activation(far_q[0:kw, :], far_qT[0:kw, bass.ds(t * P, P)], ACT.Copy).then_inc(far_q_made, 1)
                        act.wait_ge(far_masked, n + 1)
                        act.activation(far_e, far_e, ACT.Exp, bias=far_sum[:, 2:3],
                                       accum_out=far_sum[:, 0:1]).then_inc(far_exped, 1)

            act.wait_ge(flag_made, 1)
            far = act.value_load(flag[0:1, 0:1], min_val=0, max_val=1)
            for layer in range(4):
                prep(layer)
                with act.If(far == 0):
                    for u in BRANCHES[layer]:
                        for i in range(NT + 3):
                            if i < NT:
                                exp(u * NT + i)
                            finish(u, i)
                with act.Else():
                    for u in BRANCHES[layer]:
                        attend_far(u)
                        for i in range(NT + 3):
                            finish(u, i)

        @block.tensor
        def _(pe):
            pe.wait_ge(ident_made, 3)
            pe.wait_ge(w_in, W_LOADS)
            for hh in range(2):
                pe.transpose(tps[0][:, hh * P:(hh + 1) * P], wload[:, (4 + 2 * hh) * D:(6 + 2 * hh) * D], ident[:, :])
            for h in range(HEADS):
                pe.transpose(tps[1][:, h * D:(h + 1) * D], wload[0:D, (8 + 2 * h) * D:(10 + 2 * h) * D],
                             ident[0:D, 0:D])
            for i in range(2):
                pe.transpose(wps[1][:, i * NT:(i + 1) * NT], turned[0:NT, i, :], ident[0:NT, 0:NT])
            pe.transpose(wps[1][:, 2 * NT:2 * NT + HEADS], turned[0:HEADS, 2, :], ident[0:HEADS, 0:HEADS])
            pe.transpose(tps[0][:, 2 * P:2 * P + D], wload[D:P, 8 * D:10 * D], ident[D:P, D:P]).then_inc(w_turned, 1)
            pe.wait_ge(bad_made, 1)
            pe.matmul(wps[0][:, 0:1], ones[:, :], small[:, 15, 0:1], start=True, stop=True).then_inc(bad_summed, 1)

            def turn(n, t, layer):
                pe.wait_ge(h_made, 4 * layer + t // 4 + 1)
                if n >= 2:
                    pe.wait_ge(hT_made, n - 1)
                for q in range(4):
                    mm = pe.transpose(tps[t % 2][:, q * P:(q + 1) * P], H[:, t, q * P:(q + 1) * P], ident[:, :])
                mm.then_inc(h_turned, 1)

            def project(n, t, layer):
                wb = WB[layer][:, :, :, :].rearrange("p g i c -> p (g i c)")
                pe.wait_ge(hT_made, n + 1)
                for q in range(4):
                    if 4 * n + q >= 4:
                        pe.wait_ge(staged, 4 * n + q - 3)
                    pe.matmul(pps[q][:, 0:wb.shape[1]], hT[:, t % 2, q * P:(q + 1) * P], wb,
                              start=True, stop=True).then_inc(projected, 1)

            def finish(u, i):
                if 1 <= u <= HEADS and 1 <= i <= NT:
                    n = NT * (u - 1) + i - 1
                    pe.wait_ge(attended, n + 1)
                    if n >= 2:
                        pe.wait_ge(zT_made, n - 1)
                    for q in range(4):
                        mm = pe.transpose(tps[n % 2][:, q * P:(q + 1) * P],
                                          ot[:, (NT + n) % NOT, q * P:(q + 1) * P], ident[:, :])
                    mm.then_inc(z_turned, 1)
                if 1 <= u <= HEADS and 2 <= i <= NT + 1:
                    n = NT * (u - 1) + i - 2
                    pe.wait_ge(zT_leaky, n + 1)
                    if n >= 2:
                        pe.wait_ge(wo_used, n - 1)
                    for q in range(4):
                        mm = pe.matmul(wps[n % 2][:, q * P:(q + 1) * P], hT[:, n % 2, q * P:(q + 1) * P],
                                       WoB[:, u - 1, :, :].rearrange("p i c -> p (i c)"),
                                       start=True, stop=True)
                    mm.then_inc(wo_made, 1)

            def attend_far(u):
                un = UNITS[u]
                w, kw = un["w"], 2 if un["add"] else D
                keys, values, queries = (r[:, 0:NT * w].rearrange("p (t c) -> p t c", t=NT) for r in far_rows)
                if un["add"]:
                    keys, queries = far_pairs
                with pe.Fori(0, B) as b:
                    pe.wait_ge(far_source, B * u + b + 1)
                    for c in range(NT):
                        pe.matmul(pps[c // 4][0:kw, (c % 4) * P:(c % 4 + 1) * P], keys[:, c, 0:kw], ident[:, :],
                                  start=True, stop=True)
                        mm = pe.matmul((tps + wps)[c // 4][0:kw, (c % 4) * P:(c % 4 + 1) * P],
                                       queries[:, c, 0:kw], ident[:, :], start=True, stop=True)
                    mm.then_inc(far_turned, 1)
                    with pe.Fori(0, NT) as t:
                        n = NT * (B * u + b) + t
                        pe.wait_ge(far_q_made, n + 1)
                        for q in range(4):
                            mm = pe.matmul(pps[q][:, :], far_q[0:kw, :], far_kT[0:kw, q * 512:(q + 1) * 512],
                                           start=True, stop=True)
                        mm.then_inc(far_scored, 1)
                        pe.wait_ge(far_exped, n + 1)
                        for c in range(NT):
                            mm = pe.transpose(pps[c // 4][:, (c % 4) * P:(c % 4 + 1) * P],
                                              far_e[:, c * P:(c + 1) * P], ident[:, :])
                        mm.then_inc(far_p_turned, 1)
                        pe.wait_ge(far_pT_made, n + 1)
                        for c in range(NT):
                            mm = pe.matmul(tps[0][:, 0:D], far_pT[:, c * P:(c + 1) * P], values[:, c, 0:D],
                                           start=(c == 0), stop=(c == NT - 1))
                        mm.then_inc(far_summed, 1)

            pe.wait_ge(w_built, 1)
            pe.wait_ge(flag_made, 1)
            far = pe.value_load(flag[0:1, 0:1], min_val=0, max_val=1)
            for layer in range(4):
                for t in range(NT + 1):
                    if t < NT:
                        turn(NT * layer + t, t, layer)
                    if t >= 1:
                        project(NT * layer + t - 1, t - 1, layer)
                with pe.If(far == 0):
                    for u in BRANCHES[layer]:
                        for i in range(NT + 3):
                            finish(u, i)
                with pe.Else():
                    for u in BRANCHES[layer]:
                        attend_far(u)
                        for i in range(NT + 3):
                            finish(u, i)

        @block.vector
        def _(dve):
            part = ["order", 0]

            def run(ins):
                part[1] += 1
                ins.then_inc(dve_done[part[0]], 1)
                dve.wait_ge(dve_done[part[0]], part[1])

            def tell(ins, to, value):
                ins.then_inc(to, 1)
                dve.wait_ge(to, value)

            deg, key, rank, rank1 = small[:, 0, :], small[:, 2, :], small[:, 3, :], small[:, 4, :]
            diag, nvalid, nodef, cap = small[:, 5, :], small[:, 6, :], small[:, 7, :], small[:, 8, :]
            tmp, bad, tmp2 = small[:, 9, :], small[:, 10, :], small[:, 11, :]
            allbad, badflag = small[:, 15, 0:1], small[:, 14, 0:1]

            run(dve.memset(epsc[:, :], EPS))
            for s in (far_summed, far_bias_made, far_scored):
                tell(dve.memset(far_sum[:, :], 0.0), s, 1)
            dve.wait_ge(ident_made, 3)
            run(dve.tensor_scalar(other[:, :], ident[:, :], -1.0, 1.0, ALU.mult, ALU.add))
            for w in (*WB, WoB):
                run(dve.memset(w[:, :, :, :], 0.0))
            dve.wait_ge(ident_made, 3)
            dve.wait_ge(w_in, W_LOADS)
            dve.wait_ge(w_turned, 1)
            run(dve.tensor_copy(XR[:, :, E:E + 2].rearrange("p t i -> p i t"),
                                wps[1][:, 0:2 * NT].rearrange("p (i t) -> p i t", i=2)))
            run(dve.tensor_copy(bh[:, :], wps[1][:, 2 * NT:2 * NT + HEADS]))
            for i in range(2):
                lo, hi = i * D, (i + 1) * D
                run(dve.tensor_copy(WB[0][lo:hi, 0, i, 0:D], wload[lo:hi, 0:D]))
                run(dve.tensor_copy(WB[2][lo:hi, :, i, :], wload[lo:hi, D:4 * D].rearrange("p (g d) -> p g d", g=3)))
                run(dve.tensor_copy(WB[1][lo:hi, :, i, :], tps[0][lo:hi, 0:2 * P].rearrange("p (g d) -> p g d", g=HEADS)))
                run(dve.tensor_copy(WoB[lo:hi, :, i, :], tps[1][lo:hi, 0:2 * P].rearrange("p (g d) -> p g d", g=HEADS)))
                run(dve.tensor_copy(WB[3][lo:hi, 0, i, 0:D], tps[0][lo:hi, 2 * P:2 * P + D]))
                for l, wb in enumerate((WB[0], WB[3])):
                    for c, half in ((D, 1), (D + 1, 0)):
                        run(dve.tensor_tensor(wtmp[lo:hi, :], wb[lo:hi, 0, i, 0:D],
                                              abc[lo:hi, l, half * D:(half + 1) * D], ALU.mult))
                        run(dve.tensor_reduce(wb[lo:hi, 0, i, c:c + 1], wtmp[lo:hi, :], AX.X, ALU.add))
            tell(dve.memset(tmp, 0.0), w_built, 1)
            for c in range(NT):
                dve.wait_ge(adj_loaded[c % 3], 16 * (c // 3 + 1))
                tell(dve.tensor_scalar(mask[:, c, :], adjt[:, c % 3, :], 0.0, None, ALU.is_gt, ALU.add,
                                       accum_out=deg[:, c:c + 1]), adj_used, c + 1)
                run(dve.tensor_tensor_reduce(junk[:, 0:P], mask[:, c, c * P:(c + 1) * P], ident[:, :], 1.0, 0.0,
                                             ALU.mult, ALU.add, diag[:, c:c + 1]))
            dve.wait_ge(iota_made, 1)
            run(dve.tensor_copy(nodef, iot[:, :]))
            run(dve.tensor_scalar(tmp, nodef, -1.0, float(N - 1), ALU.mult, ALU.add))
            tell(dve.scalar_tensor_tensor(key, deg, float(N), tmp, ALU.mult, ALU.add), key_made, 1)
            dve.wait_ge(key_rows, 16)
            for c in range(NT):
                run(dve.tensor_scalar(junk, brow, key[:, c:c + 1], None, ALU.is_gt, ALU.add,
                                      accum_out=rank[:, c:c + 1]))
            tell(dve.tensor_scalar(rank1, rank, 1.0, None, ALU.add), rank_made, 1)
            run(dve.tensor_scalar(cap, rank, float(P * (NT - 1)), float(SLOTS[-2] - SLOTS[-1]), ALU.is_lt, ALU.mult))
            for t in range(NT - 1):
                if t < NT - 2 and SLOTS[t] > SLOTS[t + 1]:
                    run(dve.tensor_scalar(tmp, rank, float(P * (t + 1)), float(SLOTS[t] - SLOTS[t + 1]),
                                          ALU.is_lt, ALU.mult))
                    run(dve.tensor_tensor(cap, cap, tmp, ALU.add))
            run(dve.tensor_scalar(cap, cap, float(SLOTS[-1]), None, ALU.add))
            dve.wait_ge(rank_rows, 16)
            for c in range(NT):
                run(dve.tensor_tensor(ranked.rearrange("p (t q) -> p t q", t=NT),
                                      mask[:, c, :].rearrange("p (t q) -> p t q", t=NT),
                                      brow.rearrange("p (q t) -> p t q", t=NT), ALU.mult))
                for q in range(4):
                    run(dve.max(cand[:, 0, q * 8:(q + 1) * 8], ranked[:, q * (N // 4):(q + 1) * (N // 4)]))
                run(dve.max(lists[:, c, 0:8], cand[:, 0, :]))
                run(dve.match_replace(cand[:, 1, :], lists[:, c, 0:8], cand[:, 0, :], 0.0))
                run(dve.max(lists[:, c, 8:16], cand[:, 1, :]))
            run(dve.tensor_scalar(valid[:, :, :], lists[:, :, :], 0.0, None, ALU.is_gt))
            run(dve.tensor_reduce(nvalid, valid[:, :, :], AX.X, ALU.add))
            run(dve.tensor_scalar(lists[:, :, :], lists[:, :, :], -1.0, 0.0, ALU.add, ALU.max))
            run(dve.tensor_copy(XR[:, :, E + 2:E + 2 + NL].bitcast(I32), lists[:, :, :]))
            run(dve.tensor_scalar(XR[:, :, E + 2 + NL:E + 2 + 2 * NL], valid[:, :, :], -NEG, NEG, ALU.mult, ALU.add))
            run(dve.tensor_copy(XR[:, :, XS - 1].bitcast(I32), iot[:, :]))
            run(dve.tensor_tensor(bad, deg, cap, ALU.is_gt))
            run(dve.tensor_scalar(tmp, diag, 1.0, None, ALU.is_lt))
            run(dve.tensor_tensor(bad, bad, tmp, ALU.add))
            run(dve.tensor_tensor(tmp, nvalid, deg, ALU.not_equal))
            run(dve.tensor_tensor(bad, bad, tmp, ALU.add))
            tell(dve.tensor_reduce(allbad, bad, AX.X, ALU.add), bad_made, 1)
            dve.wait_ge(bad_summed, 1)
            run(dve.tensor_scalar(badflag, wps[0][:, 0:1], 0.0, None, ALU.is_gt))
            tell(dve.tensor_copy(flag[:, :], badflag), flag_made, 1)
            run(dve.tensor_tensor(tmp, nodef, rank, ALU.subtract))
            run(dve.scalar_tensor_tensor(tmp2, tmp, badflag, rank, ALU.mult, ALU.add))
            tell(dve.tensor_copy(ranki[:, :], tmp2), ordered, 1)
            dve.wait_ge(x_loaded, 16 * 5)

            def bd(ap):
                return ap.rearrange("p (b d) -> p b d", d=D)

            def over_d(ap, n):
                return ap.unsqueeze(2).to_broadcast([P, n, D])

            def prep(layer):
                part[:] = [f"prep{layer}", 0]

                def sum_squares(g):
                    dve.wait_ge(squared, 4 * layer + g + 1)
                    s = stats[:, 2, 4 * B * g:4 * B * (g + 1)]
                    tell(dve.tensor_reduce(s, bd(sq[:, g % 2, :]), AX.X, ALU.add), squares_used, 4 * layer + g + 1)

                for g in range(4):
                    xg = X[:, 4 * g:4 * g + 4, :].rearrange("p t e -> p (t e)")
                    hg = H[:, 4 * g:4 * g + 4, :].rearrange("p t e -> p (t e)")
                    s, m = (stats[:, i, 4 * B * g:4 * B * (g + 1)] for i in range(2))
                    run(dve.tensor_reduce(s, bd(xg), AX.X, ALU.add))
                    run(dve.tensor_scalar(m, s, 1.0 / D, None, ALU.mult))
                    tell(dve.tensor_tensor(bd(hg), bd(xg), over_d(m, 4 * B), ALU.subtract), centred, 4 * layer + g + 1)
                    if g >= 1:
                        sum_squares(g - 1)
                sum_squares(3)
                tell(dve.memset(mx[:, 0, 0:1], 0.0), var_made, layer + 1)
                dve.wait_ge(sd_made, layer + 1)
                run(dve.reciprocal(stats[:, 3, :], sd[:, :]))
                for g in range(4):
                    hg = H[:, 4 * g:4 * g + 4, :].rearrange("p t e -> p (t e)")
                    tell(dve.scalar_tensor_tensor(bd(hg), bd(hg), 0.0, over_d(stats[:, 3, 4 * B * g:4 * B * (g + 1)], 4 * B),
                                                  ALU.max, ALU.mult), h_made, 4 * layer + g + 1)
                tables, w = PROJ[layer]
                ng = len(tables)
                for t in range(NT):
                    n = NT * layer + t
                    before = 16 * sum(len(PROJ[l][0]) for l in range(layer)) * (NT // 2) + 16 * ng * (t // 2)
                    if before:
                        dve.wait_ge(stage_stored[t % 2], before)
                    for q in range(4):
                        dve.wait_ge(projected, 4 * n + q + 1)
                        to = stage[:, t % 2, 0:ng * B * w].rearrange("p (g c) -> p g c", g=ng)[:, :, 2 * q * w:2 * (q + 1) * w]
                        tell(dve.tensor_copy(to, pps[q][:, 0:2 * ng * w].rearrange("p (g c) -> p g c", g=ng)),
                             staged, 4 * n + q + 1)

            def score(u, t):
                un, j, K = UNITS[u], NT * u + t, SLOTS[t]
                g = BATCH_OF[u, t, un["keys"]]
                w = un["w"]
                S = sc[:, j % 2, 0:K * B].rearrange("p (k b) -> p k b", k=K)
                S2 = sc2[:, 0:K * B].rearrange("p (k b) -> p k b", k=K)
                dve.wait_ge(gathered[g % NRB], gathered_by(g))
                if un["own"] is not None:
                    o = OWN_OF[u, t]
                    dve.wait_ge(own_loaded[o % NOWN], 16 * (o // NOWN + 1))
                    mine = own[:, o % NOWN, 0:w * B]
                else:
                    mine = H[:, t, :]
                rows = rowbuf[g % NRB][:, 0:K * w * B]
                if un["add"]:
                    source = rows.rearrange("p (k b c) -> p k b c", k=K, b=B)[:, :, :, D]
                    self_ = mine.rearrange("p (b c) -> p b c", b=B)[:, :, D + 1].unsqueeze(1).to_broadcast([P, K, B])
                    tell(dve.tensor_tensor(S, source, self_, ALU.add), own_used, o + 1)
                else:
                    chunks = -(-K // CHUNK)
                    for c in range(chunks):
                        k = K * c // chunks
                        n = K * (c + 1) // chunks - k
                        pr = prod[:, 0:n * E]
                        last = k + n == K and un["own"] is not None
                        ins = dve.tensor_tensor(pr.rearrange("p (k e) -> p k e", k=n),
                                                rows.rearrange("p (k e) -> p k e", k=K)[:, k:k + n, :],
                                                mine.unsqueeze(1).to_broadcast([P, n, E]), ALU.mult)
                        if last:
                            tell(ins, own_used, o + 1)
                        else:
                            run(ins)
                        ins = dve.tensor_reduce(sc[:, j % 2, k * B:(k + n) * B], bd(pr), AX.X, ALU.add)
                        if k + n == K and un["keys"] != un["values"]:
                            tell(ins, rows_used[g % NRB], g // NRB + 1)
                        else:
                            run(ins)
                if un["slope"] is not None:
                    run(dve.scalar_tensor_tensor(S2, S, un["slope"], S, ALU.mult, ALU.max))
                else:
                    S2 = S
                mb = gbias[:, t, 0:K].unsqueeze(2).to_broadcast([P, K, B])
                run(dve.scalar_tensor_tensor(S, S2, un["factor"], mb, ALU.mult, ALU.add))
                run(dve.tensor_reduce(mx[:, 0, :], S.rearrange("p k b -> p b k"), AX.X, ALU.max))
                tell(dve.tensor_tensor(S, S, mx[:, 0, :].unsqueeze(1).to_broadcast([P, K, B]), ALU.subtract),
                     scored, j + 1)

            def attend(u, t, last):
                un, j, K = UNITS[u], NT * u + t, SLOTS[t]
                g = BATCH_OF[u, t, un["values"]]
                w = un["w"]
                S = sc[:, j % 2, 0:K * B].rearrange("p (k b) -> p k b", k=K)
                dve.wait_ge(exped, j + 1)
                run(dve.tensor_reduce(mx[:, 1, :], S.rearrange("p k b -> p b k"), AX.X, ALU.add))
                run(dve.reciprocal(mx[:, 1, :], mx[:, 1, :]))
                run(dve.tensor_tensor(S, S, mx[:, 1, :].unsqueeze(1).to_broadcast([P, K, B]), ALU.mult))
                if un["keys"] != un["values"]:
                    dve.wait_ge(gathered[g % NRB], gathered_by(g))
                v = rowbuf[g % NRB][:, 0:K * w * B].rearrange("p (k b c) -> p k b c", k=K, b=B)[:, :, :, 0:D]
                pk = S.unsqueeze(3).to_broadcast([P, K, B, D])
                run(dve.tensor_tensor(v, v, pk, ALU.mult))
                o = ot[:, j % NOT, :]
                last(dve.tensor_reduce(bd(o), v.rearrange("p k b d -> p b d k"), AX.X, ALU.add), o)

            def finish0(i):
                if 1 <= i <= NT:
                    t = i - 1
                    o, b = ot[:, t % NOT, :], bn[:, t % 2, :]
                    run(dve.bn_stats(b[:, 0:6], o))
                    tell(dve.bn_aggr(b[:, 6:8], b[:, 0:6]), bn_made, t + 1)
                if 2 <= i <= NT + 1:
                    t = i - 2
                    o, b, a = ot[:, t % NOT, :], bn[:, t % 2, :], aux[:, t % 2, :]
                    dve.wait_ge(bn_rooted, t + 1)
                    run(dve.reciprocal(b[:, 9:10], b[:, 8:9]))
                    run(dve.tensor_tensor(b[:, 10:11], b[:, 9:10], gamma[:, t, :], ALU.mult))
                    run(dve.scalar_tensor_tensor(o, o, b[:, 6:7], b[:, 10:11].to_broadcast([P, E]), ALU.subtract, ALU.mult))
                    run(dve.scalar_tensor_tensor(o, o, beta[:, t, :], H[:, t, :], ALU.add, ALU.add))
                    tell(dve.tensor_scalar(a, o, 0.0, None, ALU.min), elu_in, t + 1)
                if 3 <= i <= NT + 2:
                    t = i - 3
                    o, a = ot[:, t % NOT, :], aux[:, t % 2, :]
                    dve.wait_ge(elu_exped, t + 1)
                    run(dve.scalar_tensor_tensor(o, o, 0.0, a, ALU.max, ALU.add))
                    run(dve.scalar_tensor_tensor(X[:, t, :], o, -1.0, X[:, t, :], ALU.add, ALU.add))

            def finish_head(u, i):
                if 2 <= i <= NT + 1:
                    n = NT * (u - 1) + i - 2
                    z = hT[:, n % 2, :]
                    dve.wait_ge(zT_made, n + 1)
                    tell(dve.scalar_tensor_tensor(z, z, 0.2, z, ALU.mult, ALU.max), zT_leaky, n + 1)
                if 3 <= i <= NT + 2:
                    t, n = i - 3, NT * (u - 1) + i - 3
                    dve.wait_ge(wo_made, n + 1)
                    if u == 1:
                        ins = dve.tensor_copy(H[:, t, :], wps[n % 2][:, :])
                    else:
                        ins = dve.tensor_tensor(H[:, t, :], wps[n % 2][:, :], H[:, t, :], ALU.add)
                    tell(ins, wo_used, n + 1)

            def finish1(i):
                def feature(r):
                    return rows64[:, r, :].unsqueeze(1).to_broadcast([P, B, D])

                if 1 <= i <= NT:
                    t = i - 1
                    o = ot[:, (5 * NT + t) % NOT, :]
                    m = ln[:, 0, 0:B]
                    run(dve.tensor_tensor(bd(o), bd(o), feature(0), ALU.add))
                    run(dve.scalar_tensor_tensor(o, o, 0.2, o, ALU.mult, ALU.max))
                    run(dve.tensor_reduce(m, bd(o), AX.X, ALU.add))
                    run(dve.tensor_scalar(m, m, 1.0 / D, None, ALU.mult))
                    tell(dve.tensor_tensor(bd(o), bd(o), over_d(m, B), ALU.subtract), z_centred, t + 1)
                if 2 <= i <= NT + 1:
                    t = i - 2
                    dve.wait_ge(z_squared, t + 1)
                    tell(dve.tensor_reduce(ln[:, 2, (t % 2) * B:(t % 2 + 1) * B], bd(aux[:, t % 2, :]), AX.X, ALU.add),
                         z_var, t + 1)
                if 3 <= i <= NT + 2:
                    t = i - 3
                    o = ot[:, (5 * NT + t) % NOT, :]
                    r = ln[:, 1, 0:B]
                    dve.wait_ge(z_rooted, t + 1)
                    run(dve.reciprocal(r, ln[:, 3, (t % 2) * B:(t % 2 + 1) * B]))
                    run(dve.tensor_tensor(bd(o), bd(o), over_d(r, B), ALU.mult))
                    run(dve.tensor_tensor(bd(o), bd(o), feature(1), ALU.mult))
                    run(dve.tensor_tensor(bd(o), bd(o), feature(2), ALU.add))
                    run(dve.tensor_tensor(X[:, t, :], o, X[:, t, :], ALU.add))

            def finish(u, i):
                if u == 0:
                    finish0(i)
                elif u <= HEADS:
                    finish_head(u, i)
                elif u == 5:
                    finish1(i)
                elif 1 <= i <= NT:
                    t = i - 1
                    o = ot[:, (NT * u + t) % NOT, :]
                    if u == 6:
                        run(dve.tensor_tensor(X[:, t, :], o, X[:, t, :], ALU.add))
                    else:
                        tell(dve.scalar_tensor_tensor(X[:, t, :], o, 0.0, X[:, t, :], ALU.max, ALU.add), x_final, t + 1)

            def attend_near(u):
                for i in range(NT + 3):
                    if i < NT:
                        score(u, i)
                    if 1 <= i <= NT:
                        g = BATCH_OF[u, i - 1, UNITS[u]["values"]]
                        ot_free(u, i - 1)
                        attend(u, i - 1, lambda ins, o: tell(ins, rows_used[g % NRB], g // NRB + 1))
                        if 1 <= u <= HEADS:
                            tell(dve.memset(mx[:, 0, 0:1], 0.0), attended, NT * (u - 1) + i)
                    finish(u, i)

            def ot_free(u, t):
                m = NT * (u - 1) + t
                if 1 <= u <= HEADS and m >= NOT:
                    dve.wait_ge(z_turned, m - NOT + 1)

            def attend_far(u):
                un = UNITS[u]
                w, kw = un["w"], 2 if un["add"] else D
                keys, queries = (far_rows[i][:, 0:NT * w].rearrange("p (t c) -> p t c", t=NT) for i in (0, 2))
                ops_b = 7 + 4 * un["add"]
                ops_t = 11 + (un["slope"] is not None) + (un["layer"] in (1, 2))
                done = dve_done_far[u]
                with dve.Fori(0, B) as b:
                    m = B * u + b
                    at = [0]

                    def chain(ins, before):
                        at[0] += 1
                        ins.then_inc(done, 1)
                        dve.wait_ge(done, before + at[0])

                    before = b * (ops_b + NT * ops_t)
                    dve.wait_ge(far_loaded, 48 * (m + 1))
                    if un["add"]:
                        chain(dve.memset(far_pairs[0], 1.0), before)
                        chain(dve.memset(far_pairs[1], 1.0), before)
                        chain(dve.tensor_copy(far_pairs[0][:, :, 0], keys[:, :, D]), before)
                        chain(dve.tensor_copy(far_pairs[1][:, :, 1], queries[:, :, D + 1]), before)
                    dve.memset(far_sum[:, 1:2], 0.0).then_inc(far_source, 1)
                    dve.wait_ge(far_turned, m + 1)
                    for q in range(4):
                        chain(dve.tensor_copy(far_kT[0:kw, q * 512:(q + 1) * 512], pps[q][0:kw, :]), before)
                    for q in range(4):
                        ins = dve.tensor_copy(far_qT[0:kw, q * 512:(q + 1) * 512], (tps + wps)[q][0:kw, :])
                        if q < 3:
                            chain(ins, before)
                    ins.then_inc(far_kT_made, 1)
                    assert at[0] == ops_b
                    with dve.Fori(0, NT) as t:
                        n = NT * m + t
                        at[0] = 0
                        before = b * (ops_b + NT * ops_t) + ops_b + t * ops_t
                        dve.wait_ge(far_adj_loaded, 16 * (n + 1))
                        dve.tensor_scalar(far_bias, far_adj, 0.0, NEG, ALU.is_le, ALU.mult).then_inc(far_bias_made, 1)
                        dve.wait_ge(far_bias_made, n + 2)
                        if un["layer"] in (1, 2):
                            block_ = far_bias[:, bass.ds(t * P, P)]
                            chain(dve.scalar_tensor_tensor(block_, other[:, :], 1.0, block_, ALU.mult, ALU.mult), before)
                        dve.wait_ge(far_scored, n + 2)
                        for q in range(4):
                            chain(dve.tensor_copy(far_e[:, q * 512:(q + 1) * 512], pps[q][:, :]), before)
                        if un["slope"] is not None:
                            chain(dve.scalar_tensor_tensor(far_e, far_e, un["slope"], far_e, ALU.mult, ALU.max), before)
                        chain(dve.scalar_tensor_tensor(far_e, far_e, un["factor"], far_bias, ALU.mult, ALU.add), before)
                        chain(dve.tensor_reduce(far_sum[:, 1:2], far_e, AX.X, ALU.max), before)
                        dve.tensor_scalar(far_sum[:, 2:3], far_sum[:, 1:2], -1.0, None, ALU.mult).then_inc(far_masked, 1)
                        dve.wait_ge(far_p_turned, n + 1)
                        for q in range(4):
                            ins = dve.tensor_copy(far_pT[:, q * 512:(q + 1) * 512], pps[q][:, :])
                            if q < 3:
                                chain(ins, before)
                        ins.then_inc(far_pT_made, 1)
                        dve.wait_ge(far_summed, n + 2)
                        chain(dve.reciprocal(far_sum[:, 1:2], far_sum[:, 0:1]), before)
                        to = far_out[:, bass.ds(t, 1), bass.ds(b * D, D)].rearrange("p o d -> p (o d)")
                        chain(dve.tensor_scalar(to, tps[0][:, 0:D], far_sum[:, 1:2], None, ALU.mult), before)
                        assert at[0] == ops_t

            def finish_far(u):
                for i in range(NT + 3):
                    if 1 <= i <= NT:
                        ot_free(u, i - 1)
                        ins = dve.tensor_copy(ot[:, (NT * u + i - 1) % NOT, :], far_out[:, i - 1, :])
                        if 1 <= u <= HEADS:
                            tell(ins, attended, NT * (u - 1) + i)
                        else:
                            run(ins)
                    finish(u, i)

            far = dve.value_load(flag[0:1, 0:1], min_val=0, max_val=1)
            for layer in range(4):
                prep(layer)
                with dve.If(far == 0):
                    part[:] = [f"near{layer}", 0]
                    for u in BRANCHES[layer]:
                        attend_near(u)
                with dve.Else():
                    part[:] = [f"end{layer}", 0]
                    for u in BRANCHES[layer]:
                        attend_far(u)
                        finish_far(u)


W_LOADS = 16 * (2 * (4 + 2 + 3) + 2 + 2 + 3)

_INS = ['x', 'adj', 'L0_gnn_W', 'L0_gnn_a', 'L0_gnn_gamma', 'L0_gnn_beta', 'L1_gnn_Wh', 'L1_gnn_bh', 'L1_gnn_Wo',
        'L1_gnn_bo', 'L1_gnn_gamma', 'L1_gnn_beta', 'L2_gnn_weight', 'L2_gnn_query', 'L2_gnn_key_p', 'L3_gnn_W',
        'L3_gnn_a']


def kernel(**inputs):
    import numpy as _np
    import concourse.bacc as _bacc
    from concourse import mybir as _mybir
    from concourse.bass_utils import run_bass_kernel_spmd as _run

    nc = _bacc.Bacc("TRN2", target_bir_lowering=False, num_devices=1)
    arrays, args = {}, []
    for name in _INS:
        a = _np.ascontiguousarray(inputs[name])
        arrays[f"in_{name}"] = a
        args.append(nc.dram_tensor(f"in_{name}", a.shape, _mybir.dt.from_np(a.dtype), kind="ExternalInput").ap())
    args.append(nc.dram_tensor("out_0", (B, N, D), _mybir.dt.float32, kind="ExternalOutput").ap())
    program(nc, *args)
    r = _run(nc, [arrays], core_ids=[0])
    return r.results[0]["out_0"]
```

```python
import concourse.bass as bass
from concourse import mybir
from contextlib import ExitStack

F32 = mybir.dt.float32
BF16 = mybir.dt.bfloat16
I32 = mybir.dt.int32
ALU = mybir.AluOpType
ACT = mybir.ActivationFunctionType
AX = mybir.AxisListType

P = 128
B, N, D = 8, 2048, 64
NT = N // P
E = B * D
HEADS = 4
EPS = 1e-5
NEG = -9e15
DK = float(N) ** 0.5

SLOTS = [14, 8, 7, 7, 6, 6, 6, 5, 5, 5, 4, 4, 4, 3, 3, 2]
NL = 16
RW = D + 2
XS = E + 2 + 2 * NL + 1

H2 = -1
UNITS = ([dict(layer=0, keys=0, values=0, own=0, w=RW, slope=0.2, factor=1.0 / DK, add=True)]
         + [dict(layer=1, keys=h, values=h, own=h, w=D, slope=None, factor=1.0, add=False)
            for h in range(HEADS)]
         + [dict(layer=1, keys=H2, values=H2, own=None, w=D, slope=None, factor=1.0, add=False)]
         + [dict(layer=2, keys=0, values=1, own=2, w=D, slope=0.01, factor=1.0, add=False)]
         + [dict(layer=3, keys=0, values=0, own=0, w=RW, slope=0.2, factor=1.0, add=True)])
PROJ = [(1, RW), (HEADS, D), (3, D), (1, RW)]
BRANCHES = [[0], [1, 2, 3, 4, 5], [6], [7]]

ROWBUF = [SLOTS[0] * RW * B, SLOTS[0] * E, SLOTS[1] * E, SLOTS[1] * E]
NRB = len(ROWBUF)
CHUNK = 4
NST = 4
NOWN = 3
NSC = 3
NOT = 3


def gather_batches():
    out = []
    for u, un in enumerate(UNITS):
        for t in range(NT):
            for tab in dict.fromkeys([un["keys"], un["values"]]):
                out.append((u, t, tab, SLOTS[t]))
    return out


BATCHES = gather_batches()
BATCH_OF = {(u, t, tab): g for g, (u, t, tab, _) in enumerate(BATCHES)}


def gathered_by(g):
    return 16 * sum(BATCHES[i][3] for i in range(g % NRB, g + 1, NRB))


OWNS = [(u, t) for u, un in enumerate(UNITS) for t in range(NT) if un["own"] is not None]
OWN_OF = {ut: o for o, ut in enumerate(OWNS)}


def stored_by(layer, slot):
    return 16 * len(range(slot, 4 * NT * (layer + 1), NST))


def last_used(g):
    u, t, tab, _ = BATCHES[g - NRB]
    return tab != UNITS[u]["values"], NT * u + t


def act_slots(t):
    return SLOTS[t] // 2


LAG = {0: 3, HEADS + 1: 3, HEADS + 2: 1}
PREP = 5


def steps(u):
    return NT + (LAG[u] + PREP - 1 if u in LAG else 3)


def program(nc, x, adj, L0_W, L0_a, L0_gamma, L0_beta, L1_Wh, L1_bh, L1_Wo, L1_bo, L1_gamma, L1_beta,
            L2_weight, L2_query, L2_key, L3_W, L3_a, out):
    xs = nc.dram_tensor("xs", (N, XS), F32, kind="Internal").ap()
    keyd = nc.dram_tensor("keyd", (N,), F32, kind="Internal").ap()
    rankd = nc.dram_tensor("rankd", (N,), F32, kind="Internal").ap()
    tabs = [nc.dram_tensor(f"tab{l}", (PROJ[l][0] * N, B * PROJ[l][1]), F32, kind="Internal").ap() for l in range(4)]
    h2_table = nc.dram_tensor("h2_table", (N, E), F32, kind="Internal").ap()
    out_rows = out.rearrange("b n d -> (b n) d")

    ctx = ExitStack()
    with ctx:
        def sb(name, shape, dt=F32):
            return ctx.enter_context(nc.sbuf_tensor(name, shape, dt))

        def ps(name, shape, dt=F32):
            return ctx.enter_context(nc.psum_tensor(name, shape, dt))

        def sem(name):
            return ctx.enter_context(nc.semaphore(name))

        XH = sb("XH", [P, 2 * NT * E])
        X = XH[:, 0:NT * E].rearrange("p (t e) -> p t e", t=NT)
        H = XH[:, NT * E:].rearrange("p (t e) -> p t e", t=NT)
        mask = XH[:, :].bitcast(BF16).rearrange("p (t n) -> p t n", t=NT)[:, :, :]
        arena_w = sum(ROWBUF) + CHUNK * E
        arena = sb("arena", [P, arena_w])
        rowbuf = [arena[:, sum(ROWBUF[:i]):sum(ROWBUF[:i + 1])] for i in range(NRB)]
        prod = arena[:, sum(ROWBUF):sum(ROWBUF) + CHUNK * E]
        stage = sb("stage", [P, NST, E])
        sq = sb("sq", [P, E])
        XR = arena[:, 0:NT * XS].rearrange("p (t e) -> p t e", t=NT)
        at = NT * XS
        adjt = arena[:, at:at + 3 * N].bitcast(I32).rearrange("p (s n) -> p s n", s=3)
        at += 3 * N
        brow = arena[:, at:at + N]
        at += N
        ranked = arena[:, at:at + N]
        at += N
        junk = arena[:, at:at + N]
        assert at + N <= arena_w

        def take(width, at=[0]):
            at[0] += width
            assert at[0] <= arena_w
            return arena[:, at[0] - width:at[0]]

        far_out = take(NT * E).rearrange("p (t e) -> p t e", t=NT)
        far_rows = [take(NT * RW) for _ in range(3)]
        far_pairs = [take(NT * 2).rearrange("p (t c) -> p t c", c=2) for _ in range(2)]
        far_kT, far_qT, far_e, far_pT, far_bias = (take(N) for _ in range(5))
        far_adj = take(N).bitcast(I32)
        far_q = take(P)
        other = take(P)
        own = sb("own", [P, NOWN, RW * B])
        ot = sb("ot", [P, NOT, E])
        aux = sb("aux", [P, 2, E])
        hT = sb("hT", [P, 2, E])
        ident = sb("ident", [P, P])
        WB = [sb("WB0", [P, 1, 2, RW]), sb("WB1", [P, HEADS, 2, D]), sb("WB2", [P, 3, 2, D]),
              sb("WB3", [P, 1, 2, RW])]
        WoB = sb("WoB", [P, HEADS, 2, D])
        wload = ot[:, :, :].rearrange("p s e -> p (s e)")
        ones = own[:, 0, 0:P]
        abc = own[:, 1, 0:4 * D].rearrange("p (l o) -> p l o", l=2)
        wtmp = own[:, 2, 0:D]
        turned = aux[:, 1, 64:64 + 3 * P].rearrange("p (i c) -> p i c", i=3)
        bh = sb("bh", [P, HEADS])
        rows64 = sb("rows64", [P, 3, D])
        SI = sb("SI", [P, NT, XS - E])
        sc = sb("sc", [P, NSC, SLOTS[0] * B])
        sc2 = sb("sc2", [P, SLOTS[0] * B])
        mx = sb("mx", [P, 2, B])
        stats = sb("stats", [P, 4, NT * B])
        sd = sb("sd", [P, NT * B])
        bn = sb("bn", [P, 2, 16])
        ln = sb("ln", [P, 4, 2 * B])
        epsc = sb("epsc", [P, 1])
        far_sum = sb("far_sum", [P, 3])
        small = sb("small", [P, 16, NT])
        flag = sb("flag", [P, 1], I32)
        ranki = sb("ranki", [P, NT], I32)
        iot = sb("iot", [P, NT], I32)
        lists = aux[:, 0, 0:NT * NL].rearrange("p (t k) -> p t k", t=NT)
        valid = aux[:, 0, NT * NL:2 * NT * NL].rearrange("p (t k) -> p t k", t=NT)
        cand = aux[:, 1, 0:64].rearrange("p (i c) -> p i c", i=2)

        gbias = SI[:, :, 2 + NL:2 + 2 * NL]
        gidx = SI[:, :, 2:2 + NL].bitcast(I32)
        gamma = SI[:, :, 0:1]
        beta = SI[:, :, 1:2]
        node = SI[:, :, 2 + 2 * NL:].bitcast(I32)

        tps = [ps(f"tps{i}", [P, 512]) for i in range(2)]
        pps = [ps(f"pps{i}", [P, 512]) for i in range(4)]
        wps = [ps(f"wps{i}", [P, 512]) for i in range(2)]
        sums = pps[2:4]
        proj = pps[0:2] + wps

        adj_loaded = [sem(f"adj_loaded{i}") for i in range(3)]
        adj_used = sem("adj_used")
        x_in = sem("x_in")
        w_in = sem("w_in")
        iota_made = sem("iota_made")
        ident_made = sem("ident_made")
        key_made = sem("key_made")
        key_stored = sem("key_stored")
        key_rows = sem("key_rows")
        rank_made = sem("rank_made")
        rank_stored = sem("rank_stored")
        rank_rows = sem("rank_rows")
        bad_made = sem("bad_made")
        bad_summed = sem("bad_summed")
        flag_made = sem("flag_made")
        ordered = sem("ordered")
        scattered = sem("scattered")
        x_loaded = sem("x_loaded")
        w_turned = sem("w_turned")
        w_built = sem("w_built")
        centred = sem("centred")
        squared = sem("squared")
        var_made = sem("var_made")
        sd_made = sem("sd_made")
        h_made = sem("h_made")
        h_turned = sem("h_turned")
        hT_made = sem("hT_made")
        projected = sem("projected")
        staged = sem("staged")
        stage_stored = [sem(f"stage_stored{i}") for i in range(NST)]
        h2_stored = sem("h2_stored")
        gathered = [sem(f"gathered{i}") for i in range(NRB)]
        keys_used = sem("keys_used")
        normed = sem("normed")
        weighed = sem("weighed")
        act_weighed = sem("act_weighed")
        summed = sem("summed")
        sum_used = sem("sum_used")
        own_loaded = [sem(f"own_loaded{i}") for i in range(NOWN)]
        own_used = sem("own_used")
        scored = sem("scored")
        exped = sem("exped")
        attended = sem("attended")
        bn_made = sem("bn_made")
        bn_rooted = sem("bn_rooted")
        elu_in = sem("elu_in")
        elu_exped = sem("elu_exped")
        z_turned = sem("z_turned")
        zT_made = sem("zT_made")
        zT_leaky = sem("zT_leaky")
        wo_made = sem("wo_made")
        wo_used = sem("wo_used")
        z_centred = sem("z_centred")
        z_squared = sem("z_squared")
        z_var = sem("z_var")
        z_rooted = sem("z_rooted")
        far_loaded = sem("far_loaded")
        far_adj_loaded = sem("far_adj_loaded")
        far_source = sem("far_source")
        far_turned = sem("far_turned")
        far_kT_made = sem("far_kT_made")
        far_q_made = sem("far_q_made")
        far_bias_made = sem("far_bias_made")
        far_scored = sem("far_scored")
        far_masked = sem("far_masked")
        far_exped = sem("far_exped")
        far_p_turned = sem("far_p_turned")
        far_pT_made = sem("far_pT_made")
        far_summed = sem("far_summed")
        dve_done_far = [sem(f"dve_done_far{u}") for u in range(len(UNITS))]
        x_final = sem("x_final")
        out_stored = sem("out_stored")
        dve_done = {k: sem(f"dve_done_{k}") for k in
                    ["order", "prep", "near0", "near1", "near2", "near3",
                     "end0", "end1", "end2", "end3"]}

        block = ctx.enter_context(nc.Block())

        ADJ = adj.rearrange("(t p) n -> p t n", p=P)

        def table(u, tab):
            if tab == H2:
                return h2_table
            return tabs[UNITS[u]["layer"]][tab * N:(tab + 1) * N, :]

        def store_h2(sp, t):
            sp.wait_ge(wo_used, NT * (HEADS - 1) + t + 1)
            sp.dma_start(h2_table[t * P:(t + 1) * P, :], H[:, t, :]).then_inc(h2_stored, 16)

        def load_far(sp, u):
            un = UNITS[u]
            w = un["w"]
            queries = un["keys"] if un["own"] is None else un["own"]
            with sp.Fori(0, B) as b:
                sp.wait_ge(far_summed, NT * (B * u + b) + 1)
                for to, tab in zip(far_rows, (un["keys"], un["values"], queries)):
                    rows = table(u, tab).rearrange("(t p) (b c) -> p t b c", p=P, b=B)
                    sp.dma_start(to[:, 0:NT * w].rearrange("p (t c) -> p t c", t=NT).unsqueeze(2),
                                 rows[:, :, bass.ds(b, 1), :]).then_inc(far_loaded, 16)
                with sp.Fori(0, NT) as t:
                    sp.wait_ge(far_bias_made, NT * (B * u + b) + t + 1)
                    sp.dma_start(far_adj, ADJ[:, bass.ds(t, 1), :].rearrange("p o n -> p (o n)"))\
                      .then_inc(far_adj_loaded, 16)

        @block.sync
        def _(sp):
            for c in range(NT):
                if c >= 3:
                    sp.wait_ge(adj_used, c - 2)
                sp.dma_start(adjt[:, c % 3, :], ADJ[:, c, :]).then_inc(adj_loaded[c % 3], 16)
            sp.wait_ge(key_made, 1)
            sp.dma_start(keyd.rearrange("(p t) -> p t", p=P), small[:, 2, :]).then_inc(key_stored, 16)
            sp.wait_ge(key_stored, 16)
            sp.dma_start(brow, keyd.partition_broadcast(P)).then_inc(key_rows, 16)
            sp.wait_ge(rank_made, 1)
            sp.dma_start(rankd.rearrange("(p t) -> p t", p=P), small[:, 4, :]).then_inc(rank_stored, 16)
            sp.wait_ge(rank_stored, 16)
            sp.dma_start(brow, rankd.partition_broadcast(P)).then_inc(rank_rows, 16)
            sp.wait_ge(scattered, 16 * NT)
            XSV = xs.rearrange("(t p) e -> p t e", p=P)
            sp.dma_start(SI[:, :, :], XSV[:, :, E:]).then_inc(x_loaded, 16)
            for t in range(0, NT, 4):
                sp.dma_start(X[:, t:t + 4, :], XSV[:, t:t + 4, 0:E]).then_inc(x_loaded, 16)

            def load_own(u, t):
                o = OWN_OF[u, t]
                w = UNITS[u]["w"] * B
                if o >= NOWN:
                    sp.wait_ge(own_used, o - NOWN + 1)
                tab = UNITS[u]["own"]
                sp.dma_start(own[:, o % NOWN, 0:w],
                             table(u, tab)[t * P:(t + 1) * P, :])\
                  .then_inc(own_loaded[o % NOWN], 16)

            def store(layer, t):
                ng, w = PROJ[layer]
                for q in range(4):
                    m = 4 * (NT * layer + t) + q
                    to = tabs[layer][0:ng * N, :].rearrange("(g t p) e -> t p g e", g=ng, p=P)
                    sp.wait_ge(staged, m + 1)
                    sp.dma_start(to[t, :, :, 2 * q * w:2 * (q + 1) * w],
                                 stage[:, m % NST, 0:2 * ng * w].rearrange("p (g c) -> p g c", g=ng))\
                      .then_inc(stage_stored[m % NST], 16)

            def all_stored(layer):
                for i in range(NST):
                    sp.wait_ge(stage_stored[i], stored_by(layer, i))

            sp.wait_ge(flag_made, 1)
            far = sp.value_load(flag[0:1, 0:1], min_val=0, max_val=1)
            for t in range(NT):
                store(0, t)
            for layer in range(4):
                all_stored(layer)
                with sp.If(far == 0):
                    for u in BRANCHES[layer]:
                        has_own = UNITS[u]["own"] is not None
                        if has_own:
                            load_own(u, 0)
                            load_own(u, 1)
                        for i in range(steps(u) + 2):
                            if has_own and i + 2 < NT:
                                load_own(u, i + 2)
                            if u == HEADS and 5 <= i < NT + 5:
                                store_h2(sp, i - 5)
                            if u in LAG and 0 <= i - LAG[u] - 6 < NT:
                                store(layer + 1, i - LAG[u] - 6)
                with sp.Else():
                    for u in BRANCHES[layer]:
                        if UNITS[u]["own"] is None:
                            sp.wait_ge(h2_stored, 16 * NT)
                        load_far(sp, u)
                        for i in range(steps(u)):
                            if u == HEADS and 3 <= i < NT + 3:
                                store_h2(sp, i - 3)
                            if u in LAG and 0 <= i - LAG[u] - 4 < NT:
                                store(layer + 1, i - LAG[u] - 4)
            sp.wait_ge(out_stored, 16 * B * NT)

        @block.gpsimd
        def _(pool):
            pool.memset(ident[:, :], 0.0).then_inc(ident_made, 1)
            pool.memset(ones[:, :], 1.0).then_inc(ident_made, 1)
            pool.wait_ge(ident_made, 2)
            pool.affine_select(out=ident[:, :], in_=ident[:, :], compare_op=ALU.not_equal, fill=1.0, base=0,
                               pattern=[[-1, P]], channel_multiplier=1).then_inc(ident_made, 1)
            pool.iota(iot[:, :], pattern=[[P, NT]], base=0, channel_multiplier=1).then_inc(iota_made, 1)
            pool.wait_ge(ordered, 1)
            pool.wait_ge(x_in, 16 * NT)
            for t in range(NT):
                pool.indirect_dma_start(out=xs, out_offset=bass.IndirectOffsetOnAxis(ap=ranki[:, t:t + 1], axis=0),
                                        in_=XR[:, t, :], in_offset=None).then_inc(scattered, 16)

            def gather(u, t):
                for tab in dict.fromkeys([UNITS[u]["keys"], UNITS[u]["values"]]):
                    g = BATCH_OF[u, t, tab]
                    w = UNITS[u]["w"] * B
                    if g >= NRB:
                        scores_only, j = last_used(g)
                        if scores_only:
                            pool.wait_ge(keys_used, j - NT * (HEADS + 2) + 1)
                        else:
                            pool.wait_ge(summed, j + 1)
                    for k in range(SLOTS[t]):
                        pool.indirect_dma_start(
                            out=rowbuf[g % NRB][:, k * w:(k + 1) * w], out_offset=None,
                            in_=h2_table if tab == H2 else tabs[UNITS[u]["layer"]],
                            element_offset=0 if tab == H2 else tab * N * w,
                            in_offset=bass.IndirectOffsetOnAxis(ap=gidx[:, t, k:k + 1], axis=0)
                        ).then_inc(gathered[g % NRB], 16)

            def put_out(t):
                pool.wait_ge(x_final, t + 1)
                for b in range(B):
                    pool.indirect_dma_start(
                        out=out_rows, out_offset=bass.IndirectOffsetOnAxis(ap=node[:, t, :], axis=0),
                        in_=X[:, t, b * D:(b + 1) * D], in_offset=None, element_offset=b * N * D
                    ).then_inc(out_stored, 16)

            pool.wait_ge(x_loaded, 16 * 5)
            pool.wait_ge(flag_made, 1)
            far = pool.value_load(flag[0:1, 0:1], min_val=0, max_val=1)
            with pool.If(far == 0):
                for layer in range(4):
                    for i in range(NST):
                        pool.wait_ge(stage_stored[i], stored_by(layer, i))
                    for u in BRANCHES[layer]:
                        if UNITS[u]["own"] is None:
                            pool.wait_ge(h2_stored, 16 * NT)
                        for t in range(NT):
                            gather(u, t)
                            if layer == 3 and t >= NRB:
                                put_out(t - NRB)
                for t in range(NT - NRB, NT):
                    put_out(t)
            with pool.Else():
                for t in range(NT):
                    put_out(t)

        @block.scalar
        def _(act):
            for t in range(NT):
                act.dma_start(XR[:, t, 0:E].rearrange("p (b d) -> p b d", b=B),
                              x[:, t * P:(t + 1) * P, :].rearrange("b n d -> n b d")).then_inc(x_in, 16)
            for i in range(2):
                for q, w in enumerate([L0_W, L2_key, L2_weight, L2_query]):
                    act.dma_start(wload[i * D:(i + 1) * D, q * D:(q + 1) * D], w).then_inc(w_in, 16)
                for hh in range(2):
                    act.dma_start(wload[:, (4 + 2 * hh + i) * D:(5 + 2 * hh + i) * D],
                                  L1_Wh.rearrange("h d c -> (h d) c")[hh * P:(hh + 1) * P, :]).then_inc(w_in, 16)
                act.dma_start(wload[0:D, 8 * D:16 * D].rearrange("p (h i d) -> p h i d", h=HEADS, i=2)[:, :, i, :],
                              L1_Wo.rearrange("o (h d) -> o h d", h=HEADS)).then_inc(w_in, 16)
                act.dma_start(wload[D:P, (8 + i) * D:(9 + i) * D], L3_W).then_inc(w_in, 16)
                act.dma_start(turned[0:HEADS, 2, i * D:(i + 1) * D], L1_bh).then_inc(w_in, 16)
            act.dma_start(turned[0:NT, 0, :], L0_gamma.rearrange("(t p) -> t p", p=P)).then_inc(w_in, 16)
            act.dma_start(turned[0:NT, 1, :], L0_beta.rearrange("(t p) -> t p", p=P)).then_inc(w_in, 16)
            act.dma_start(abc[:, 0, :], L0_a.rearrange("a o -> (a o)").partition_broadcast(P)).then_inc(w_in, 16)
            act.dma_start(abc[:, 1, :], L3_a.rearrange("a o -> (a o)").partition_broadcast(P)).then_inc(w_in, 16)
            for i, v in enumerate([L1_bo, L1_gamma, L1_beta]):
                act.dma_start(rows64[:, i, :], v.partition_broadcast(P)).then_inc(w_in, 16)

            def prepare(layer, s):
                if 0 <= s < NT:
                    n = NT * layer + s
                    act.wait_ge(centred, n + 1)
                    if n >= 1:
                        act.wait_ge(var_made, n)
                    act.activation(sq[:, :], H[:, s, :], ACT.Square).then_inc(squared, 1)
                if 0 <= s - 1 < NT:
                    n, v = NT * layer + s - 1, slice(B * (s - 1), B * s)
                    act.wait_ge(var_made, n + 1)
                    act.activation(sd[:, v], stats[:, 2, v], ACT.Sqrt, bias=epsc[:, 0:1], scale=1.0 / D)\
                       .then_inc(sd_made, 1)
                if 0 <= s - 3 < NT:
                    n = NT * layer + s - 3
                    act.wait_ge(h_turned, n + 1)
                    act.activation(hT[:, n % 2, :], tps[n % 2][:, :], ACT.Copy).then_inc(hT_made, 1)
                if 0 <= s - 4 < NT:
                    ng, w = PROJ[layer]
                    for q in range(4):
                        m = 4 * (NT * layer + s - 4) + q
                        act.wait_ge(projected, m + 1)
                        if m >= NST:
                            act.wait_ge(stage_stored[m % NST], 16 * (m // NST))
                        act.activation(stage[:, m % NST, 0:2 * ng * w], proj[q][:, 0:2 * ng * w],
                                       ACT.Copy).then_inc(staged, 1)

            def exp(j):
                act.wait_ge(scored, j + 1)
                w = SLOTS[j % NT] * B
                act.activation(sc[:, j % NSC, 0:w], sc[:, j % NSC, 0:w], ACT.Exp).then_inc(exped, 1)

            def weigh(u, t):
                un, j, K, w = UNITS[u], NT * u + t, SLOTS[t], UNITS[u]["w"]
                g = BATCH_OF[u, t, un["values"]]
                rows = rowbuf[g % NRB][:, 0:K * w * B].rearrange("p (k b c) -> p k b c", k=K, b=B)
                act.wait_ge(normed, j + 1)
                act.wait_ge(gathered[g % NRB], gathered_by(g))
                for k in range(K - act_slots(t), K):
                    for b in range(B):
                        v = rows[:, k, b, 0:D]
                        ins = act.activation(v, v, ACT.Copy, scale=sc[:, j % NSC, k * B + b:k * B + b + 1])
                ins.then_inc(act_weighed, 1)

            def take_out(u, t):
                j = NT * u + t
                act.wait_ge(summed, j + 1)
                m = NT * (u - 1) + t
                if u == 0 and t >= NOT:
                    act.wait_ge(centred, NT + t - NOT + 1)
                if u > 0 and m >= NOT:
                    act.wait_ge(z_turned, m - NOT + 1)
                act.activation(ot[:, j % NOT, :], sums[j % 2][:, :], ACT.Copy).then_inc(attended, 1)

            def finish(u, i):
                if u == 0 and 1 <= i <= NT:
                    act.wait_ge(bn_made, i)
                    act.activation(bn[:, (i - 1) % 2, 8:9], bn[:, (i - 1) % 2, 7:8], ACT.Sqrt,
                                   bias=epsc[:, 0:1]).then_inc(bn_rooted, 1)
                if u == 0 and 2 <= i <= NT + 1:
                    t = i - 2
                    act.wait_ge(elu_in, t + 1)
                    act.activation(aux[:, t % 2, :], aux[:, t % 2, :], ACT.Exp).then_inc(elu_exped, 1)
                if 1 <= u <= HEADS and 1 <= i <= NT:
                    h, n = u - 1, NT * (u - 1) + i - 1
                    act.wait_ge(z_turned, n + 1)
                    if n >= 2:
                        act.wait_ge(wo_made, n - 1)
                    act.activation(hT[:, n % 2, :], tps[n % 2][:, :], ACT.Identity,
                                   bias=bh[:, h:h + 1]).then_inc(zT_made, 1)
                if u == 5 and 1 <= i <= NT:
                    t = i - 1
                    act.wait_ge(z_centred, t + 1)
                    act.activation(aux[:, t % 2, :], ot[:, (5 * NT + t) % NOT, :], ACT.Square).then_inc(z_squared, 1)
                if u == 5 and 2 <= i <= NT + 1:
                    t = i - 2
                    act.wait_ge(z_var, t + 1)
                    act.activation(ln[:, 3, (t % 2) * B:(t % 2 + 1) * B], ln[:, 2, (t % 2) * B:(t % 2 + 1) * B],
                                   ACT.Sqrt, bias=epsc[:, 0:1], scale=1.0 / D).then_inc(z_rooted, 1)

            def attend_far(u):
                kw = 2 if UNITS[u]["add"] else D
                with act.Fori(0, B) as b:
                    act.wait_ge(far_kT_made, B * u + b + 1)
                    with act.Fori(0, NT) as t:
                        n = NT * (B * u + b) + t
                        act.wait_ge(far_scored, n + 1)
                        act.activation(far_q[0:kw, :], far_qT[0:kw, bass.ds(t * P, P)], ACT.Copy).then_inc(far_q_made, 1)
                        act.wait_ge(far_masked, n + 1)
                        act.activation(far_e, far_e, ACT.Exp, bias=far_sum[:, 2:3],
                                       accum_out=far_sum[:, 0:1]).then_inc(far_exped, 1)

            for s in range(NT + PREP - 1):
                prepare(0, s)
            act.wait_ge(flag_made, 1)
            far = act.value_load(flag[0:1, 0:1], min_val=0, max_val=1)
            for layer in range(4):
                with act.If(far == 0):
                    for u in BRANCHES[layer]:
                        for i in range(steps(u) + 2):
                            if 1 <= i <= NT:
                                exp(u * NT + i - 1)
                                weigh(u, i - 1)
                            if u <= HEADS and 2 <= i <= NT + 1:
                                take_out(u, i - 2)
                            finish(u, i - 2)
                            if u in LAG:
                                prepare(layer + 1, i - 2 - LAG[u])
                with act.Else():
                    for u in BRANCHES[layer]:
                        attend_far(u)
                        for i in range(steps(u)):
                            finish(u, i)
                            if u in LAG:
                                prepare(layer + 1, i - LAG[u])

        @block.tensor
        def _(pe):
            pe.wait_ge(ident_made, 3)
            pe.wait_ge(w_in, W_LOADS)
            for hh in range(2):
                pe.transpose(tps[0][:, hh * P:(hh + 1) * P], wload[:, (4 + 2 * hh) * D:(6 + 2 * hh) * D], ident[:, :])
            for h in range(HEADS):
                pe.transpose(tps[1][:, h * D:(h + 1) * D], wload[0:D, (8 + 2 * h) * D:(10 + 2 * h) * D],
                             ident[0:D, 0:D])
            for i in range(2):
                pe.transpose(wps[1][:, i * NT:(i + 1) * NT], turned[0:NT, i, :], ident[0:NT, 0:NT])
            pe.transpose(wps[1][:, 2 * NT:2 * NT + HEADS], turned[0:HEADS, 2, :], ident[0:HEADS, 0:HEADS])
            pe.transpose(tps[0][:, 2 * P:2 * P + D], wload[D:P, 8 * D:10 * D], ident[D:P, D:P]).then_inc(w_turned, 1)
            pe.wait_ge(bad_made, 1)
            pe.matmul(wps[0][:, 0:1], ones[:, :], small[:, 15, 0:1], start=True, stop=True).then_inc(bad_summed, 1)

            def prepare(layer, s):
                if 0 <= s - 2 < NT:
                    n = NT * layer + s - 2
                    pe.wait_ge(h_made, n + 1)
                    if n >= 2:
                        pe.wait_ge(hT_made, n - 1)
                    for q in range(4):
                        mm = pe.transpose(tps[n % 2][:, q * P:(q + 1) * P], H[:, s - 2, q * P:(q + 1) * P], ident[:, :])
                    mm.then_inc(h_turned, 1)
                if 0 <= s - 3 < NT:
                    n = NT * layer + s - 3
                    wb = WB[layer][:, :, :, :].rearrange("p g i c -> p (g i c)")
                    pe.wait_ge(hT_made, n + 1)
                    for q in range(4):
                        m = 4 * n + q
                        if m >= 4:
                            pe.wait_ge(staged, m - 3)
                        pe.matmul(proj[q][:, 0:wb.shape[1]], hT[:, n % 2, q * P:(q + 1) * P], wb,
                                  start=True, stop=True).then_inc(projected, 1)

            def add_up(u, t):
                j, K, w = NT * u + t, SLOTS[t], UNITS[u]["w"]
                g = BATCH_OF[u, t, UNITS[u]["values"]]
                rows = rowbuf[g % NRB][:, 0:K * w * B].rearrange("p (k b c) -> p k b c", k=K, b=B)
                before = j - 2
                if 0 <= before < NT * (HEADS + 1):
                    pe.wait_ge(attended, before + 1)
                elif 0 <= before < NT * (HEADS + 3):
                    pe.wait_ge(sum_used, before - NT * (HEADS + 1) + 1)
                elif before >= 0:
                    pe.wait_ge(x_final, before - NT * (HEADS + 3) + 1)
                pe.wait_ge(weighed, j + 1)
                pe.wait_ge(act_weighed, j + 1)
                to = sums[j % 2][:, :].rearrange("p (b d) -> p b d", b=B)
                for k in range(K):
                    mm = pe.matmul(to, ident[:, :], rows[:, k, :, 0:D], start=(k == 0), stop=(k == K - 1))
                mm.then_inc(summed, 1)

            def finish(u, i):
                if 1 <= u <= HEADS and 1 <= i <= NT:
                    n = NT * (u - 1) + i - 1
                    pe.wait_ge(attended, NT + n + 1)
                    if n >= 2:
                        pe.wait_ge(zT_made, n - 1)
                    for q in range(4):
                        mm = pe.transpose(tps[n % 2][:, q * P:(q + 1) * P],
                                          ot[:, (NT + n) % NOT, q * P:(q + 1) * P], ident[:, :])
                    mm.then_inc(z_turned, 1)
                if 1 <= u <= HEADS and 2 <= i <= NT + 1:
                    n = NT * (u - 1) + i - 2
                    pe.wait_ge(zT_leaky, n + 1)
                    if n >= 2:
                        pe.wait_ge(wo_used, n - 1)
                    for q in range(4):
                        mm = pe.matmul(wps[n % 2][:, q * P:(q + 1) * P], hT[:, n % 2, q * P:(q + 1) * P],
                                       WoB[:, u - 1, :, :].rearrange("p i c -> p (i c)"),
                                       start=True, stop=True)
                    mm.then_inc(wo_made, 1)

            def attend_far(u):
                un = UNITS[u]
                w, kw = un["w"], 2 if un["add"] else D
                keys, values, queries = (r[:, 0:NT * w].rearrange("p (t c) -> p t c", t=NT) for r in far_rows)
                if un["add"]:
                    keys, queries = far_pairs
                with pe.Fori(0, B) as b:
                    pe.wait_ge(far_source, B * u + b + 1)
                    for c in range(NT):
                        pe.matmul(pps[c // 4][0:kw, (c % 4) * P:(c % 4 + 1) * P], keys[:, c, 0:kw], ident[:, :],
                                  start=True, stop=True)
                        mm = pe.matmul((tps + wps)[c // 4][0:kw, (c % 4) * P:(c % 4 + 1) * P],
                                       queries[:, c, 0:kw], ident[:, :], start=True, stop=True)
                    mm.then_inc(far_turned, 1)
                    with pe.Fori(0, NT) as t:
                        n = NT * (B * u + b) + t
                        pe.wait_ge(far_q_made, n + 1)
                        for q in range(4):
                            mm = pe.matmul(pps[q][:, :], far_q[0:kw, :], far_kT[0:kw, q * 512:(q + 1) * 512],
                                           start=True, stop=True)
                        mm.then_inc(far_scored, 1)
                        pe.wait_ge(far_exped, n + 1)
                        for c in range(NT):
                            mm = pe.transpose(pps[c // 4][:, (c % 4) * P:(c % 4 + 1) * P],
                                              far_e[:, c * P:(c + 1) * P], ident[:, :])
                        mm.then_inc(far_p_turned, 1)
                        pe.wait_ge(far_pT_made, n + 1)
                        for c in range(NT):
                            mm = pe.matmul(tps[0][:, 0:D], far_pT[:, c * P:(c + 1) * P], values[:, c, 0:D],
                                           start=(c == 0), stop=(c == NT - 1))
                        mm.then_inc(far_summed, 1)

            pe.wait_ge(w_built, 1)
            for i in range(NT + PREP - 1):
                prepare(0, i)
            pe.wait_ge(flag_made, 1)
            far = pe.value_load(flag[0:1, 0:1], min_val=0, max_val=1)
            for layer in range(4):
                with pe.If(far == 0):
                    for u in BRANCHES[layer]:
                        for i in range(steps(u) + 2):
                            finish(u, i - 2)
                            if u in LAG:
                                prepare(layer + 1, i - 2 - LAG[u])
                            if 1 <= i <= NT:
                                add_up(u, i - 1)
                with pe.Else():
                    for u in BRANCHES[layer]:
                        attend_far(u)
                        for i in range(steps(u)):
                            finish(u, i)
                            if u in LAG:
                                prepare(layer + 1, i - LAG[u])

        @block.vector
        def _(dve):
            part = ["order", 0]

            def run(ins):
                part[1] += 1
                ins.then_inc(dve_done[part[0]], 1)
                dve.wait_ge(dve_done[part[0]], part[1])

            def tell(ins, to, value):
                ins.then_inc(to, 1)
                dve.wait_ge(to, value)

            deg, key, rank, rank1 = small[:, 0, :], small[:, 2, :], small[:, 3, :], small[:, 4, :]
            diag, nvalid, nodef, cap = small[:, 5, :], small[:, 6, :], small[:, 7, :], small[:, 8, :]
            tmp, bad, tmp2 = small[:, 9, :], small[:, 10, :], small[:, 11, :]
            allbad, badflag = small[:, 15, 0:1], small[:, 14, 0:1]

            run(dve.memset(epsc[:, :], EPS))
            for s in (far_summed, far_bias_made, far_scored):
                tell(dve.memset(far_sum[:, :], 0.0), s, 1)
            for w in (*WB, WoB):
                run(dve.memset(w[:, :, :, :], 0.0))
            dve.wait_ge(ident_made, 3)
            dve.wait_ge(w_in, W_LOADS)
            dve.wait_ge(w_turned, 1)
            run(dve.tensor_copy(XR[:, :, E:E + 2].rearrange("p t i -> p i t"),
                                wps[1][:, 0:2 * NT].rearrange("p (i t) -> p i t", i=2)))
            run(dve.tensor_copy(bh[:, :], wps[1][:, 2 * NT:2 * NT + HEADS]))
            for i in range(2):
                lo, hi = i * D, (i + 1) * D
                run(dve.tensor_copy(WB[0][lo:hi, 0, i, 0:D], wload[lo:hi, 0:D]))
                run(dve.tensor_copy(WB[2][lo:hi, :, i, :], wload[lo:hi, D:4 * D].rearrange("p (g d) -> p g d", g=3)))
                run(dve.tensor_copy(WB[1][lo:hi, :, i, :], tps[0][lo:hi, 0:2 * P].rearrange("p (g d) -> p g d", g=HEADS)))
                run(dve.tensor_copy(WoB[lo:hi, :, i, :], tps[1][lo:hi, 0:2 * P].rearrange("p (g d) -> p g d", g=HEADS)))
                run(dve.tensor_copy(WB[3][lo:hi, 0, i, 0:D], tps[0][lo:hi, 2 * P:2 * P + D]))
                for l, wb in enumerate((WB[0], WB[3])):
                    for c, half in ((D, 1), (D + 1, 0)):
                        run(dve.tensor_tensor(wtmp[lo:hi, :], wb[lo:hi, 0, i, 0:D],
                                              abc[lo:hi, l, half * D:(half + 1) * D], ALU.mult))
                        run(dve.tensor_reduce(wb[lo:hi, 0, i, c:c + 1], wtmp[lo:hi, :], AX.X, ALU.add))
            tell(dve.memset(tmp, 0.0), w_built, 1)
            for c in range(NT):
                dve.wait_ge(adj_loaded[c % 3], 16 * (c // 3 + 1))
                tell(dve.tensor_scalar(mask[:, c, :], adjt[:, c % 3, :], 0.0, None, ALU.is_gt, ALU.add,
                                       accum_out=deg[:, c:c + 1]), adj_used, c + 1)
                run(dve.tensor_tensor_reduce(junk[:, 0:P], mask[:, c, c * P:(c + 1) * P], ident[:, :], 1.0, 0.0,
                                             ALU.mult, ALU.add, diag[:, c:c + 1]))
            dve.wait_ge(iota_made, 1)
            run(dve.tensor_copy(nodef, iot[:, :]))
            run(dve.tensor_scalar(tmp, nodef, -1.0, float(N - 1), ALU.mult, ALU.add))
            tell(dve.scalar_tensor_tensor(key, deg, float(N), tmp, ALU.mult, ALU.add), key_made, 1)
            dve.wait_ge(key_rows, 16)
            for c in range(NT):
                run(dve.tensor_scalar(junk, brow, key[:, c:c + 1], None, ALU.is_gt, ALU.add,
                                      accum_out=rank[:, c:c + 1]))
            tell(dve.tensor_scalar(rank1, rank, 1.0, None, ALU.add), rank_made, 1)
            run(dve.tensor_scalar(cap, rank, float(P * (NT - 1)), float(SLOTS[-2] - SLOTS[-1]), ALU.is_lt, ALU.mult))
            for t in range(NT - 1):
                if t < NT - 2 and SLOTS[t] > SLOTS[t + 1]:
                    run(dve.tensor_scalar(tmp, rank, float(P * (t + 1)), float(SLOTS[t] - SLOTS[t + 1]),
                                          ALU.is_lt, ALU.mult))
                    run(dve.tensor_tensor(cap, cap, tmp, ALU.add))
            run(dve.tensor_scalar(cap, cap, float(SLOTS[-1]), None, ALU.add))
            dve.wait_ge(rank_rows, 16)
            for c in range(NT):
                run(dve.tensor_tensor(ranked.rearrange("p (t q) -> p t q", t=NT),
                                      mask[:, c, :].rearrange("p (t q) -> p t q", t=NT),
                                      brow.rearrange("p (q t) -> p t q", t=NT), ALU.mult))
                for q in range(4):
                    run(dve.max(cand[:, 0, q * 8:(q + 1) * 8], ranked[:, q * (N // 4):(q + 1) * (N // 4)]))
                run(dve.max(lists[:, c, 0:8], cand[:, 0, :]))
                run(dve.match_replace(cand[:, 1, :], lists[:, c, 0:8], cand[:, 0, :], 0.0))
                run(dve.max(lists[:, c, 8:16], cand[:, 1, :]))
            run(dve.tensor_scalar(valid[:, :, :], lists[:, :, :], 0.0, None, ALU.is_gt))
            run(dve.tensor_reduce(nvalid, valid[:, :, :], AX.X, ALU.add))
            run(dve.tensor_scalar(lists[:, :, :], lists[:, :, :], -1.0, 0.0, ALU.add, ALU.max))
            run(dve.tensor_copy(XR[:, :, E + 2:E + 2 + NL].bitcast(I32), lists[:, :, :]))
            run(dve.tensor_scalar(XR[:, :, E + 2 + NL:E + 2 + 2 * NL], valid[:, :, :], -NEG, NEG, ALU.mult, ALU.add))
            run(dve.tensor_copy(XR[:, :, XS - 1].bitcast(I32), iot[:, :]))
            run(dve.tensor_tensor(bad, deg, cap, ALU.is_gt))
            run(dve.tensor_scalar(tmp, diag, 1.0, None, ALU.is_lt))
            run(dve.tensor_tensor(bad, bad, tmp, ALU.add))
            run(dve.tensor_tensor(tmp, nvalid, deg, ALU.not_equal))
            run(dve.tensor_tensor(bad, bad, tmp, ALU.add))
            tell(dve.tensor_reduce(allbad, bad, AX.X, ALU.add), bad_made, 1)
            dve.wait_ge(bad_summed, 1)
            run(dve.tensor_scalar(badflag, wps[0][:, 0:1], 0.0, None, ALU.is_gt))
            tell(dve.tensor_copy(flag[:, :], badflag), flag_made, 1)
            run(dve.tensor_tensor(tmp, nodef, rank, ALU.subtract))
            run(dve.scalar_tensor_tensor(tmp2, tmp, badflag, rank, ALU.mult, ALU.add))
            tell(dve.tensor_copy(ranki[:, :], tmp2), ordered, 1)
            dve.wait_ge(x_loaded, 16 * 5)

            def bd(ap):
                return ap.rearrange("p (b d) -> p b d", d=D)

            def over_d(ap, n):
                return ap.unsqueeze(2).to_broadcast([P, n, D])

            def prepare(layer, s):
                if 0 <= s < NT:
                    n, v = NT * layer + s, slice(B * s, B * (s + 1))
                    run(dve.tensor_reduce(stats[:, 0, v], bd(X[:, s, :]), AX.X, ALU.add))
                    run(dve.tensor_scalar(stats[:, 1, v], stats[:, 0, v], 1.0 / D, None, ALU.mult))
                    tell(dve.tensor_tensor(bd(H[:, s, :]), bd(X[:, s, :]), over_d(stats[:, 1, v], B), ALU.subtract),
                         centred, n + 1)
                if 0 <= s - 1 < NT:
                    n, v = NT * layer + s - 1, slice(B * (s - 1), B * s)
                    dve.wait_ge(squared, n + 1)
                    tell(dve.tensor_reduce(stats[:, 2, v], bd(sq[:, :]), AX.X, ALU.add), var_made, n + 1)
                if 0 <= s - 2 < NT:
                    t, n, v = s - 2, NT * layer + s - 2, slice(B * (s - 2), B * (s - 1))
                    dve.wait_ge(sd_made, n + 1)
                    run(dve.reciprocal(stats[:, 3, v], sd[:, v]))
                    tell(dve.scalar_tensor_tensor(bd(H[:, t, :]), bd(H[:, t, :]), 0.0, over_d(stats[:, 3, v], B),
                                                  ALU.max, ALU.mult), h_made, n + 1)

            def score(u, t):
                un, j, K = UNITS[u], NT * u + t, SLOTS[t]
                g = BATCH_OF[u, t, un["keys"]]
                w = un["w"]
                S = sc[:, j % NSC, 0:K * B].rearrange("p (k b) -> p k b", k=K)
                S2 = sc2[:, 0:K * B].rearrange("p (k b) -> p k b", k=K)
                if j >= NSC:
                    dve.wait_ge(act_weighed, j - NSC + 1)
                dve.wait_ge(gathered[g % NRB], gathered_by(g))
                if un["own"] is not None:
                    o = OWN_OF[u, t]
                    dve.wait_ge(own_loaded[o % NOWN], 16 * (o // NOWN + 1))
                    mine = own[:, o % NOWN, 0:w * B]
                else:
                    mine = H[:, t, :]
                rows = rowbuf[g % NRB][:, 0:K * w * B]
                if un["add"]:
                    source = rows.rearrange("p (k b c) -> p k b c", k=K, b=B)[:, :, :, D]
                    self_ = mine.rearrange("p (b c) -> p b c", b=B)[:, :, D + 1].unsqueeze(1).to_broadcast([P, K, B])
                    tell(dve.tensor_tensor(S, source, self_, ALU.add), own_used, o + 1)
                else:
                    chunks = -(-K // CHUNK)
                    for c in range(chunks):
                        k = K * c // chunks
                        n = K * (c + 1) // chunks - k
                        pr = prod[:, 0:n * E]
                        last = k + n == K and un["own"] is not None
                        ins = dve.tensor_tensor(pr.rearrange("p (k e) -> p k e", k=n),
                                                rows.rearrange("p (k e) -> p k e", k=K)[:, k:k + n, :],
                                                mine.unsqueeze(1).to_broadcast([P, n, E]), ALU.mult)
                        if last:
                            tell(ins, own_used, o + 1)
                        else:
                            run(ins)
                        ins = dve.tensor_reduce(sc[:, j % NSC, k * B:(k + n) * B], bd(pr), AX.X, ALU.add)
                        if k + n == K and un["keys"] != un["values"]:
                            tell(ins, keys_used, t + 1)
                        else:
                            run(ins)
                if un["slope"] is not None:
                    run(dve.scalar_tensor_tensor(S2, S, un["slope"], S, ALU.mult, ALU.max))
                else:
                    S2 = S
                mb = gbias[:, t, 0:K].unsqueeze(2).to_broadcast([P, K, B])
                run(dve.scalar_tensor_tensor(S, S2, un["factor"], mb, ALU.mult, ALU.add))
                run(dve.tensor_reduce(mx[:, 0, :], S.rearrange("p k b -> p b k"), AX.X, ALU.max))
                tell(dve.tensor_tensor(S, S, mx[:, 0, :].unsqueeze(1).to_broadcast([P, K, B]), ALU.subtract),
                     scored, j + 1)

            def attend(u, t):
                un, j, K, w = UNITS[u], NT * u + t, SLOTS[t], UNITS[u]["w"]
                g = BATCH_OF[u, t, un["values"]]
                S = sc[:, j % NSC, 0:K * B].rearrange("p (k b) -> p k b", k=K)
                dve.wait_ge(exped, j + 1)
                run(dve.tensor_reduce(mx[:, 1, :], S.rearrange("p k b -> p b k"), AX.X, ALU.add))
                run(dve.reciprocal(mx[:, 1, :], mx[:, 1, :]))
                tell(dve.tensor_tensor(S, S, mx[:, 1, :].unsqueeze(1).to_broadcast([P, K, B]), ALU.mult),
                     normed, j + 1)
                if un["keys"] != un["values"]:
                    dve.wait_ge(gathered[g % NRB], gathered_by(g))
                n = K - act_slots(t)
                v = rowbuf[g % NRB][:, 0:n * w * B].rearrange("p (k b c) -> p k b c", k=n, b=B)[:, :, :, 0:D]
                tell(dve.tensor_tensor(v, v, S[:, 0:n, :].unsqueeze(3).to_broadcast([P, n, B, D]), ALU.mult),
                     weighed, j + 1)

            near = [True]

            def output(u, t):
                j = NT * u + t
                if u <= HEADS:
                    dve.wait_ge(attended, j + 1)
                elif near[0]:
                    dve.wait_ge(summed, j + 1)
                    return sums[j % 2][:, :]
                return ot[:, j % NOT, :]

            def finish0(i):
                if 1 <= i <= NT:
                    t = i - 1
                    o, b = output(0, t), bn[:, t % 2, :]
                    run(dve.bn_stats(b[:, 0:6], o))
                    tell(dve.bn_aggr(b[:, 6:8], b[:, 0:6]), bn_made, t + 1)
                if 2 <= i <= NT + 1:
                    t = i - 2
                    o, b, a = ot[:, t % NOT, :], bn[:, t % 2, :], aux[:, t % 2, :]
                    dve.wait_ge(bn_rooted, t + 1)
                    run(dve.reciprocal(b[:, 9:10], b[:, 8:9]))
                    run(dve.tensor_tensor(b[:, 10:11], b[:, 9:10], gamma[:, t, :], ALU.mult))
                    run(dve.scalar_tensor_tensor(o, o, b[:, 6:7], b[:, 10:11].to_broadcast([P, E]), ALU.subtract, ALU.mult))
                    run(dve.scalar_tensor_tensor(o, o, beta[:, t, :], H[:, t, :], ALU.add, ALU.add))
                    tell(dve.tensor_scalar(a, o, 0.0, None, ALU.min), elu_in, t + 1)
                if 3 <= i <= NT + 2:
                    t = i - 3
                    o, a = ot[:, t % NOT, :], aux[:, t % 2, :]
                    dve.wait_ge(elu_exped, t + 1)
                    run(dve.scalar_tensor_tensor(o, o, 0.0, a, ALU.max, ALU.add))
                    run(dve.scalar_tensor_tensor(X[:, t, :], o, -1.0, X[:, t, :], ALU.add, ALU.add))

            def finish_head(u, i):
                if 2 <= i <= NT + 1:
                    n = NT * (u - 1) + i - 2
                    z = hT[:, n % 2, :]
                    dve.wait_ge(zT_made, n + 1)
                    tell(dve.scalar_tensor_tensor(z, z, 0.2, z, ALU.mult, ALU.max), zT_leaky, n + 1)
                if 3 <= i <= NT + 2:
                    t, n = i - 3, NT * (u - 1) + i - 3
                    dve.wait_ge(wo_made, n + 1)
                    if u == 1:
                        ins = dve.tensor_copy(H[:, t, :], wps[n % 2][:, :])
                    else:
                        ins = dve.tensor_tensor(H[:, t, :], wps[n % 2][:, :], H[:, t, :], ALU.add)
                    tell(ins, wo_used, n + 1)

            def finish1(i):
                def feature(r):
                    return rows64[:, r, :].unsqueeze(1).to_broadcast([P, B, D])

                if 1 <= i <= NT:
                    t = i - 1
                    o = ot[:, (5 * NT + t) % NOT, :]
                    m = ln[:, 0, 0:B]
                    tell(dve.tensor_tensor(bd(o), bd(output(HEADS + 1, t)), feature(0), ALU.add), sum_used, t + 1)
                    run(dve.scalar_tensor_tensor(o, o, 0.2, o, ALU.mult, ALU.max))
                    run(dve.tensor_reduce(m, bd(o), AX.X, ALU.add))
                    run(dve.tensor_scalar(m, m, 1.0 / D, None, ALU.mult))
                    tell(dve.tensor_tensor(bd(o), bd(o), over_d(m, B), ALU.subtract), z_centred, t + 1)
                if 2 <= i <= NT + 1:
                    t = i - 2
                    dve.wait_ge(z_squared, t + 1)
                    tell(dve.tensor_reduce(ln[:, 2, (t % 2) * B:(t % 2 + 1) * B], bd(aux[:, t % 2, :]), AX.X, ALU.add),
                         z_var, t + 1)
                if 3 <= i <= NT + 2:
                    t = i - 3
                    o = ot[:, (5 * NT + t) % NOT, :]
                    r = ln[:, 1, 0:B]
                    dve.wait_ge(z_rooted, t + 1)
                    run(dve.reciprocal(r, ln[:, 3, (t % 2) * B:(t % 2 + 1) * B]))
                    run(dve.tensor_tensor(bd(o), bd(o), over_d(r, B), ALU.mult))
                    run(dve.tensor_tensor(bd(o), bd(o), feature(1), ALU.mult))
                    run(dve.tensor_tensor(bd(o), bd(o), feature(2), ALU.add))
                    run(dve.tensor_tensor(X[:, t, :], o, X[:, t, :], ALU.add))

            def finish(u, i):
                if u == 0:
                    finish0(i)
                elif u <= HEADS:
                    finish_head(u, i)
                elif u == HEADS + 1:
                    finish1(i)
                elif 1 <= i <= NT:
                    t = i - 1
                    o = output(u, t)
                    if u == HEADS + 2:
                        tell(dve.tensor_tensor(X[:, t, :], o, X[:, t, :], ALU.add), sum_used, NT + t + 1)
                    else:
                        tell(dve.scalar_tensor_tensor(X[:, t, :], o, 0.0, X[:, t, :], ALU.max, ALU.add), x_final, t + 1)

            def attend_near(u):
                for i in range(steps(u) + 2):
                    finish(u, i - 2)
                    if u in LAG:
                        prepare(UNITS[u]["layer"] + 1, i - 2 - LAG[u])
                    if 1 <= i <= NT:
                        attend(u, i - 1)
                    if i < NT:
                        score(u, i)

            def attend_far(u):
                un = UNITS[u]
                w, kw = un["w"], 2 if un["add"] else D
                keys, queries = (far_rows[i][:, 0:NT * w].rearrange("p (t c) -> p t c", t=NT) for i in (0, 2))
                ops_b = 7 + 4 * un["add"]
                ops_t = 11 + (un["slope"] is not None) + (un["layer"] in (1, 2))
                done = dve_done_far[u]
                with dve.Fori(0, B) as b:
                    m = B * u + b
                    at = [0]

                    def chain(ins, before):
                        at[0] += 1
                        ins.then_inc(done, 1)
                        dve.wait_ge(done, before + at[0])

                    before = b * (ops_b + NT * ops_t)
                    dve.wait_ge(far_loaded, 48 * (m + 1))
                    if un["add"]:
                        chain(dve.memset(far_pairs[0], 1.0), before)
                        chain(dve.memset(far_pairs[1], 1.0), before)
                        chain(dve.tensor_copy(far_pairs[0][:, :, 0], keys[:, :, D]), before)
                        chain(dve.tensor_copy(far_pairs[1][:, :, 1], queries[:, :, D + 1]), before)
                    dve.memset(far_sum[:, 1:2], 0.0).then_inc(far_source, 1)
                    dve.wait_ge(far_turned, m + 1)
                    for q in range(4):
                        chain(dve.tensor_copy(far_kT[0:kw, q * 512:(q + 1) * 512], pps[q][0:kw, :]), before)
                    for q in range(4):
                        ins = dve.tensor_copy(far_qT[0:kw, q * 512:(q + 1) * 512], (tps + wps)[q][0:kw, :])
                        if q < 3:
                            chain(ins, before)
                    ins.then_inc(far_kT_made, 1)
                    assert at[0] == ops_b
                    with dve.Fori(0, NT) as t:
                        n = NT * m + t
                        at[0] = 0
                        before = b * (ops_b + NT * ops_t) + ops_b + t * ops_t
                        dve.wait_ge(far_adj_loaded, 16 * (n + 1))
                        dve.tensor_scalar(far_bias, far_adj, 0.0, NEG, ALU.is_le, ALU.mult).then_inc(far_bias_made, 1)
                        dve.wait_ge(far_bias_made, n + 2)
                        if un["layer"] in (1, 2):
                            block_ = far_bias[:, bass.ds(t * P, P)]
                            chain(dve.scalar_tensor_tensor(block_, other, 1.0, block_, ALU.mult, ALU.mult), before)
                        dve.wait_ge(far_scored, n + 2)
                        for q in range(4):
                            chain(dve.tensor_copy(far_e[:, q * 512:(q + 1) * 512], pps[q][:, :]), before)
                        if un["slope"] is not None:
                            chain(dve.scalar_tensor_tensor(far_e, far_e, un["slope"], far_e, ALU.mult, ALU.max), before)
                        chain(dve.scalar_tensor_tensor(far_e, far_e, un["factor"], far_bias, ALU.mult, ALU.add), before)
                        chain(dve.tensor_reduce(far_sum[:, 1:2], far_e, AX.X, ALU.max), before)
                        dve.tensor_scalar(far_sum[:, 2:3], far_sum[:, 1:2], -1.0, None, ALU.mult).then_inc(far_masked, 1)
                        dve.wait_ge(far_p_turned, n + 1)
                        for q in range(4):
                            ins = dve.tensor_copy(far_pT[:, q * 512:(q + 1) * 512], pps[q][:, :])
                            if q < 3:
                                chain(ins, before)
                        ins.then_inc(far_pT_made, 1)
                        dve.wait_ge(far_summed, n + 2)
                        chain(dve.reciprocal(far_sum[:, 1:2], far_sum[:, 0:1]), before)
                        to = far_out[:, bass.ds(t, 1), bass.ds(b * D, D)].rearrange("p o d -> p (o d)")
                        chain(dve.tensor_scalar(to, tps[0][:, 0:D], far_sum[:, 1:2], None, ALU.mult), before)
                        assert at[0] == ops_t

            def finish_far(u):
                for i in range(steps(u)):
                    if 1 <= i <= NT:
                        m = NT * (u - 1) + i - 1
                        if 1 <= u <= HEADS and m >= NOT:
                            dve.wait_ge(z_turned, m - NOT + 1)
                        ins = dve.tensor_copy(ot[:, (NT * u + i - 1) % NOT, :], far_out[:, i - 1, :])
                        if u <= HEADS:
                            tell(ins, attended, NT * u + i)
                        else:
                            run(ins)
                    finish(u, i)
                    if u in LAG:
                        prepare(UNITS[u]["layer"] + 1, i - LAG[u])

            part[:] = ["prep", 0]
            for i in range(NT + PREP - 1):
                prepare(0, i)
            far = dve.value_load(flag[0:1, 0:1], min_val=0, max_val=1)
            for layer in range(4):
                with dve.If(far == 0):
                    part[:] = [f"near{layer}", 0]
                    near[0] = True
                    for u in BRANCHES[layer]:
                        attend_near(u)
                with dve.Else():
                    part[:] = [f"end{layer}", 0]
                    near[0] = False
                    run(dve.tensor_scalar(other, ident[:, :], -1.0, 1.0, ALU.mult, ALU.add))
                    for u in BRANCHES[layer]:
                        attend_far(u)
                        finish_far(u)


W_LOADS = 16 * (2 * (4 + 2 + 3) + 2 + 2 + 3)

_INS = ['x', 'adj', 'L0_gnn_W', 'L0_gnn_a', 'L0_gnn_gamma', 'L0_gnn_beta', 'L1_gnn_Wh', 'L1_gnn_bh', 'L1_gnn_Wo',
        'L1_gnn_bo', 'L1_gnn_gamma', 'L1_gnn_beta', 'L2_gnn_weight', 'L2_gnn_query', 'L2_gnn_key_p', 'L3_gnn_W',
        'L3_gnn_a']


def kernel(**inputs):
    import numpy as _np
    import concourse.bacc as _bacc
    from concourse import mybir as _mybir
    from concourse.bass_utils import run_bass_kernel_spmd as _run

    nc = _bacc.Bacc("TRN2", target_bir_lowering=False, num_devices=1)
    arrays, args = {}, []
    for name in _INS:
        a = _np.ascontiguousarray(inputs[name])
        arrays[f"in_{name}"] = a
        args.append(nc.dram_tensor(f"in_{name}", a.shape, _mybir.dt.from_np(a.dtype), kind="ExternalInput").ap())
    args.append(nc.dram_tensor("out_0", (B, N, D), _mybir.dt.float32, kind="ExternalOutput").ap())
    program(nc, *args)
    r = _run(nc, [arrays], core_ids=[0])
    return r.results[0]["out_0"]
```

```python
import concourse.bass as bass
from concourse import mybir
from contextlib import ExitStack

F32 = mybir.dt.float32
F16 = mybir.dt.float16
I32 = mybir.dt.int32
ALU = mybir.AluOpType
ACT = mybir.ActivationFunctionType
AX = mybir.AxisListType

P = 128
B, N, D = 8, 2048, 64
NT = N // P
E = B * D
HEADS = 4
EPS = 1e-5
NEG = -9e15
DK = float(N) ** 0.5

BY_RANK = [13, 8, 7, 7, 6, 6, 5, 5, 5, 5, 4, 4, 4, 3, 3, 2]
PLACE_OF = [8, 4, 5, 6, 7, 9, 10, 11, 12, 13, 14, 15, 3, 2, 1, 0]
SLOTS = [BY_RANK[PLACE_OF.index(t)] for t in range(NT)]
NL = 16
RW = D + 2
XS = E + 2 + 2 * NL + 1

H2 = -1
UNITS = ([dict(layer=0, keys=0, values=0, own=0, w=RW, slope=0.2, factor=1.0 / DK, add=True)]
         + [dict(layer=1, keys=h, values=h, own=h, w=D, slope=None, factor=1.0, add=False)
            for h in range(HEADS)]
         + [dict(layer=1, keys=H2, values=H2, own=None, w=D, slope=None, factor=1.0, add=False)]
         + [dict(layer=2, keys=0, values=1, own=2, w=D, slope=0.01, factor=1.0, add=False)]
         + [dict(layer=3, keys=0, values=0, own=0, w=RW, slope=0.2, factor=1.0, add=True)])
PROJ = [(1, RW), (HEADS, D), (3, D), (1, RW)]
BRANCHES = [[[0]], [[1, 2, 3, 4], [5]], [[6]], [[7]]]

ROWBUF = [BY_RANK[0] * RW * B, BY_RANK[0] * E, BY_RANK[1] * E, BY_RANK[1] * E]
NRB = len(ROWBUF)
CHUNK = 6
AHEAD = 2
NST = 4
NOWN = 3
NSC = 3
NOT = 3


def gather_batches():
    out = []
    for u, un in enumerate(UNITS):
        for t in range(NT):
            for tab in dict.fromkeys([un["keys"], un["values"]]):
                out.append((u, t, tab, SLOTS[t]))
    return out


BATCHES = gather_batches()
BATCH_OF = {(u, t, tab): g for g, (u, t, tab, _) in enumerate(BATCHES)}
assert all(K * UNITS[u]["w"] * B <= ROWBUF[g % NRB] for g, (u, _, _, K) in enumerate(BATCHES))


def gathered_by(g):
    return 16 * sum(BATCHES[i][3] for i in range(g % NRB, g + 1, NRB))


OWNS = [(u, t) for u, un in enumerate(UNITS) for t in range(NT) if un["own"] is not None]
OWN_OF = {ut: o for o, ut in enumerate(OWNS)}


def stored_by(layer, slot):
    return 16 * len(range(slot, 4 * NT * (layer + 1), NST))


def last_used(g):
    u, t, tab, _ = BATCHES[g - NRB]
    return tab != UNITS[u]["values"], NT * u + t


def act_slots(u, t):
    return max(1, SLOTS[t] // 4) if UNITS[u]["add"] else min((SLOTS[t] + 1) // 2, ACT_MOST)


def folded(u, t):
    return (SLOTS[t] - act_slots(u, t)) // 3 if UNITS[u]["add"] else 0


ACT_MOST = 4
ACT_RANKS = 10
POOL_RANKED = [c for c in range(NT) if c % 4]

LAG = {0: 3, HEADS + 1: 4, HEADS + 2: 1}
PREP = 5


def steps(u):
    return NT + (LAG[u] + PREP - 1 if u in LAG else 5)


def near_steps(group):
    for s in range(NT * (len(group) - 1) + steps(group[-1]) + 2):
        yield [(u, s - NT * k) for k, u in enumerate(group) if 0 <= s - NT * k < steps(u) + 2]


def program(nc, x, adj, L0_W, L0_a, L0_gamma, L0_beta, L1_Wh, L1_bh, L1_Wo, L1_bo, L1_gamma, L1_beta,
            L2_weight, L2_query, L2_key, L3_W, L3_a, out):
    xs = nc.dram_tensor("xs", (N, XS), F32, kind="Internal").ap()
    keyd = nc.dram_tensor("keyd", (N,), F32, kind="Internal").ap()
    placed = nc.dram_tensor("placed", (N,), F32, kind="Internal").ap()
    tabs = [nc.dram_tensor(f"tab{l}", (PROJ[l][0] * N, B * PROJ[l][1]), F32, kind="Internal").ap() for l in range(4)]
    h2_table = nc.dram_tensor("h2_table", (N, E), F32, kind="Internal").ap()
    finished = nc.dram_tensor("finished", (N, E), F32, kind="Internal").ap()

    ctx = ExitStack()
    with ctx:
        def sb(name, shape, dt=F32):
            return ctx.enter_context(nc.sbuf_tensor(name, shape, dt))

        def ps(name, shape, dt=F32):
            return ctx.enter_context(nc.psum_tensor(name, shape, dt))

        def sem(name):
            return ctx.enter_context(nc.semaphore(name))

        XH = sb("XH", [P, 2 * NT * E])
        X = XH[:, 0:NT * E].rearrange("p (t e) -> p t e", t=NT)
        H = XH[:, NT * E:].rearrange("p (t e) -> p t e", t=NT)
        mask = XH[:, :].bitcast(F16).rearrange("p (t n) -> p t n", t=NT)
        arena_w = sum(ROWBUF) + CHUNK * E
        arena = sb("arena", [P, arena_w])
        rowbuf = [arena[:, sum(ROWBUF[:i]):sum(ROWBUF[:i + 1])] for i in range(NRB)]
        prod = arena[:, sum(ROWBUF):sum(ROWBUF) + CHUNK * E]
        stage = sb("stage", [P, NST, E])
        sq = sb("sq", [P, E])
        XR = arena[:, 0:NT * XS].rearrange("p (t e) -> p t e", t=NT)
        at = NT * XS
        adjt = arena[:, at:at + 3 * N].bitcast(I32).rearrange("p (s n) -> p s n", s=3)
        at += 3 * N
        brow = arena[:, at:at + N]
        at += N
        places, dve_ranked = (arena[:, at + i * N // 2:at + (i + 1) * N // 2].bitcast(F16) for i in range(2))
        at += N
        pool_ranked = [adjt[:, i, 0:N // 2].bitcast(F16) for i in range(3)]
        junk = arena[:, at:at + N]
        at += N
        act_junk = arena[:, at:at + N]
        assert at + N <= arena_w

        def take(width, at=[0]):
            at[0] += width
            assert at[0] <= arena_w
            return arena[:, at[0] - width:at[0]]

        far_out = take(NT * E).rearrange("p (t e) -> p t e", t=NT)
        far_rows = [take(NT * RW) for _ in range(3)]
        far_pairs = [take(NT * 2).rearrange("p (t c) -> p t c", c=2) for _ in range(2)]
        far_kT, far_qT, far_e, far_pT, far_bias = (take(N) for _ in range(5))
        far_adj = take(N).bitcast(I32)
        far_q = take(P)
        other = take(P)
        own = sb("own", [P, NOWN, RW * B])
        ot = sb("ot", [P, NOT, E])
        aux = sb("aux", [P, 2, E])
        hT = sb("hT", [P, 2, E])
        ident = sb("ident", [P, P])
        WB = [sb("WB0", [P, 1, 2, RW]), sb("WB1", [P, HEADS, 2, D]), sb("WB2", [P, 3, 2, D]),
              sb("WB3", [P, 1, 2, RW])]
        WoB = sb("WoB", [P, HEADS, 2, D])
        wload = ot[:, :, :].rearrange("p s e -> p (s e)")
        ones = own[:, 0, 0:P]
        abc = own[:, 1, 0:4 * D].rearrange("p (l o) -> p l o", l=2)
        wtmp = own[:, 2, 0:D]
        turned = aux[:, 1, 64:64 + 3 * P].rearrange("p (i c) -> p i c", i=3)
        bh = sb("bh", [P, 2 * HEADS])
        rows64 = sb("rows64", [P, 3, D])
        SI = sb("SI", [P, NT, XS - E])
        sc = sb("sc", [P, NSC, BY_RANK[0] * B])
        sc2 = sb("sc2", [P, BY_RANK[0] * B])
        mx = sb("mx", [P, 2, B])
        stats = sb("stats", [P, 4, NT * B])
        sd = sb("sd", [P, NT * B])
        bn = sb("bn", [P, 2, 16])
        ln = sb("ln", [P, 4, 2 * B])
        epsc = sb("epsc", [P, 1])
        far_sum = sb("far_sum", [P, 3])
        small = sb("small", [P, 16, NT])
        flag = sb("flag", [P, 1], I32)
        placei = sb("placei", [P, NT], I32)
        iot = sb("iot", [P, NT], I32)
        lists = aux[:, 0, 0:NT * NL].rearrange("p (t k) -> p t k", t=NT)
        valid = aux[:, 0, NT * NL:2 * NT * NL].rearrange("p (t k) -> p t k", t=NT)
        cand = aux[:, 1, 0:64].rearrange("p (i c) -> p i c", i=2)

        negkey, signs = small[:, 12, :], small[:, 13, :]
        gbias = SI[:, :, 2 + NL:2 + 2 * NL]
        gidx = SI[:, :, 2:2 + NL].bitcast(I32)
        gamma = SI[:, :, 0:1]
        beta = SI[:, :, 1:2]
        node = SI[:, :, 2 + 2 * NL:].bitcast(I32)

        tps = [ps(f"tps{i}", [P, 512]) for i in range(2)]
        pps = [ps(f"pps{i}", [P, 512]) for i in range(4)]
        wps = [ps(f"wps{i}", [P, 512]) for i in range(2)]
        sums = pps[2:4]
        proj = pps[0:2] + wps

        adj_loaded = [sem(f"adj_loaded{i}") for i in range(3)]
        adj_used = sem("adj_used")
        x_in = sem("x_in")
        w_in = sem("w_in")
        iota_made = sem("iota_made")
        ident_made = sem("ident_made")
        key_made = sem("key_made")
        key_stored = sem("key_stored")
        key_rows = sem("key_rows")
        sign_made = sem("sign_made")
        signs_summed = sem("signs_summed")
        place_made = sem("place_made")
        place_stored = sem("place_stored")
        place_rows = sem("place_rows")
        places_made = sem("places_made")
        ranked_made = sem("ranked_made")
        ranked_used = sem("ranked_used")
        bad_made = sem("bad_made")
        bad_summed = sem("bad_summed")
        flag_made = sem("flag_made")
        ordered = sem("ordered")
        scattered = sem("scattered")
        info_loaded = sem("info_loaded")
        x_loaded = [sem(f"x_loaded{i}") for i in range(4)]
        w_turned = sem("w_turned")
        w_built = sem("w_built")
        mean_made = sem("mean_made")
        centred = sem("centred")
        squared = sem("squared")
        var_made = sem("var_made")
        sd_made = sem("sd_made")
        h_made = sem("h_made")
        h_turned = sem("h_turned")
        hT_made = sem("hT_made")
        projected = sem("projected")
        staged = sem("staged")
        stage_stored = [sem(f"stage_stored{i}") for i in range(NST)]
        h2_stored = sem("h2_stored")
        gathered = [sem(f"gathered{i}") for i in range(NRB)]
        keys_used = sem("keys_used")
        normed = sem("normed")
        weighed = sem("weighed")
        act_weighed = sem("act_weighed")
        summed = sem("summed")
        sum_used = sem("sum_used")
        own_loaded = [sem(f"own_loaded{i}") for i in range(NOWN)]
        own_used = sem("own_used")
        scored = sem("scored")
        exped = sem("exped")
        attended = sem("attended")
        bn_made = sem("bn_made")
        bn_rooted = sem("bn_rooted")
        elu_in = sem("elu_in")
        elu_exped = sem("elu_exped")
        z_turned = sem("z_turned")
        zT_made = sem("zT_made")
        zT_leaky = sem("zT_leaky")
        wo_made = sem("wo_made")
        wo_out = sem("wo_out")
        h2_summed = sem("h2_summed")
        z_centred = sem("z_centred")
        z_squared = sem("z_squared")
        z_var = sem("z_var")
        z_rooted = sem("z_rooted")
        far_loaded = sem("far_loaded")
        far_adj_loaded = sem("far_adj_loaded")
        far_source = sem("far_source")
        far_turned = sem("far_turned")
        far_kT_made = sem("far_kT_made")
        far_q_made = sem("far_q_made")
        far_bias_made = sem("far_bias_made")
        far_scored = sem("far_scored")
        far_masked = sem("far_masked")
        far_exped = sem("far_exped")
        far_p_turned = sem("far_p_turned")
        far_pT_made = sem("far_pT_made")
        far_summed = sem("far_summed")
        dve_done_far = [sem(f"dve_done_far{u}") for u in range(len(UNITS))]
        z_mean = sem("z_mean")
        z_inverse = sem("z_inverse")
        z_affine = sem("z_affine")
        x1_made = sem("x1_made")
        x_final = sem("x_final")
        put_in_order = sem("put_in_order")
        out_stored = sem("out_stored")
        dve_done = {k: sem(f"dve_done_{k}") for k in
                    ["order", "prep", "near0", "near1", "near2", "near3",
                     "end0", "end1", "end2", "end3"]}

        block = ctx.enter_context(nc.Block())

        ADJ = adj.rearrange("(t p) n -> p t n", p=P)

        def table(u, tab):
            if tab == H2:
                return h2_table
            return tabs[UNITS[u]["layer"]][tab * N:(tab + 1) * N, :]

        def bd(ap):
            return ap.rearrange("p (b d) -> p b d", d=D)

        def over_d(ap, n):
            return ap.unsqueeze(2).to_broadcast([P, n, D])

        def feature(r):
            return rows64[:, r, :].unsqueeze(1).to_broadcast([P, B, D])

        def store_h2(sp, t):
            sp.wait_ge(h2_summed, NT * (HEADS - 2) + t + 1)
            sp.dma_start(h2_table[t * P:(t + 1) * P, :], H[:, t, :]).then_inc(h2_stored, 16)

        def load_far(sp, u):
            un = UNITS[u]
            w = un["w"]
            queries = un["keys"] if un["own"] is None else un["own"]
            with sp.Fori(0, B) as b:
                sp.wait_ge(far_summed, NT * (B * u + b) + 1)
                for to, tab in zip(far_rows, (un["keys"], un["values"], queries)):
                    rows = table(u, tab).rearrange("(t p) (b c) -> p t b c", p=P, b=B)
                    sp.dma_start(to[:, 0:NT * w].rearrange("p (t c) -> p t c", t=NT).unsqueeze(2),
                                 rows[:, :, bass.ds(b, 1), :]).then_inc(far_loaded, 16)
                with sp.Fori(0, NT) as t:
                    sp.wait_ge(far_bias_made, NT * (B * u + b) + t + 1)
                    sp.dma_start(far_adj, ADJ[:, bass.ds(t, 1), :].rearrange("p o n -> p (o n)"))\
                      .then_inc(far_adj_loaded, 16)

        @block.sync
        def _(sp):
            for c in range(NT):
                if c >= 3:
                    sp.wait_ge(adj_used, c - 2)
                sp.dma_start(adjt[:, c % 3, :], ADJ[:, c, :]).then_inc(adj_loaded[c % 3], 16)
            sp.wait_ge(key_made, 1)
            sp.dma_start(keyd.rearrange("(p t) -> p t", p=P), small[:, 2, :]).then_inc(key_stored, 16)
            sp.wait_ge(key_stored, 16)
            sp.dma_start(brow, keyd.partition_broadcast(P)).then_inc(key_rows, 16)
            sp.wait_ge(place_made, 1)
            sp.dma_start(placed.rearrange("(p t) -> p t", p=P), small[:, 4, :]).then_inc(place_stored, 16)
            sp.wait_ge(place_stored, 16)
            sp.dma_start(brow, placed.partition_broadcast(P)).then_inc(place_rows, 16)
            sp.wait_ge(scattered, 16 * NT)
            XSV = xs.rearrange("(t p) e -> p t e", p=P)
            sp.dma_start(SI[:, :, :], XSV[:, :, E:]).then_inc(info_loaded, 16)
            for i in range(4):
                sp.dma_start(X[:, 4 * i:4 * i + 4, :], XSV[:, 4 * i:4 * i + 4, 0:E]).then_inc(x_loaded[i], 16)

            def load_own(u, t):
                o = OWN_OF[u, t]
                w = UNITS[u]["w"] * B
                if o >= NOWN:
                    sp.wait_ge(own_used, o - NOWN + 1)
                tab = UNITS[u]["own"]
                sp.dma_start(own[:, o % NOWN, 0:w],
                             table(u, tab)[t * P:(t + 1) * P, :])\
                  .then_inc(own_loaded[o % NOWN], 16)

            def store(layer, t):
                ng, w = PROJ[layer]
                for q in range(4):
                    m = 4 * (NT * layer + t) + q
                    to = tabs[layer][0:ng * N, :].rearrange("(g t p) e -> t p g e", g=ng, p=P)
                    sp.wait_ge(staged, m + 1)
                    sp.dma_start(to[t, :, :, 2 * q * w:2 * (q + 1) * w],
                                 stage[:, m % NST, 0:2 * ng * w].rearrange("p (g c) -> p g c", g=ng))\
                      .then_inc(stage_stored[m % NST], 16)

            def all_stored(layer):
                for i in range(NST):
                    sp.wait_ge(stage_stored[i], stored_by(layer, i))

            sp.wait_ge(flag_made, 1)
            far = sp.value_load(flag[0:1, 0:1], min_val=0, max_val=1)
            for t in range(NT):
                store(0, t)
            for layer in range(4):
                all_stored(layer)
                with sp.If(far == 0):
                    for group in BRANCHES[layer]:
                        owns = [(u, t) for u in group for t in range(NT) if UNITS[u]["own"] is not None]
                        for ut in owns[:2]:
                            load_own(*ut)
                        for s, step in enumerate(near_steps(group)):
                            if s + 2 < len(owns):
                                load_own(*owns[s + 2])
                            for u, i in step:
                                if u == HEADS and 7 <= i < NT + 7:
                                    store_h2(sp, i - 7)
                                if u in LAG and 0 <= i - LAG[u] - 6 < NT:
                                    store(layer + 1, i - LAG[u] - 6)
                with sp.Else():
                    for u in sum(BRANCHES[layer], []):
                        if UNITS[u]["own"] is None:
                            sp.wait_ge(h2_stored, 16 * NT)
                        load_far(sp, u)
                        for i in range(steps(u)):
                            if u == HEADS and 5 <= i < NT + 5:
                                store_h2(sp, i - 5)
                            if u in LAG and 0 <= i - LAG[u] - 4 < NT:
                                store(layer + 1, i - LAG[u] - 4)
            sp.wait_ge(put_in_order, 16 * NT)
            for b in range(B):
                sp.dma_start(out[b, :, :], finished[:, b * D:(b + 1) * D]).then_inc(out_stored, 16)
            sp.wait_ge(out_stored, 16 * B)

        @block.gpsimd
        def _(pool):
            pool.memset(ident[:, :], 0.0).then_inc(ident_made, 1)
            pool.memset(ones[:, :], 1.0).then_inc(ident_made, 1)
            pool.wait_ge(ident_made, 2)
            pool.affine_select(out=ident[:, :], in_=ident[:, :], compare_op=ALU.not_equal, fill=1.0, base=0,
                               pattern=[[-1, P]], channel_multiplier=1).then_inc(ident_made, 1)
            pool.iota(iot[:, :], pattern=[[P, NT]], base=0, channel_multiplier=1).then_inc(iota_made, 1)
            pool.wait_ge(places_made, 1)
            for i, c in enumerate(POOL_RANKED):
                if i >= 3:
                    pool.wait_ge(ranked_used, i - 2)
                pool.tensor_tensor(pool_ranked[i % 3], mask[:, c, :], places, ALU.mult).then_inc(ranked_made, 1)
            pool.wait_ge(ordered, 1)
            pool.wait_ge(x_in, 16 * NT)
            for t in range(NT):
                pool.indirect_dma_start(out=xs, out_offset=bass.IndirectOffsetOnAxis(ap=placei[:, t:t + 1], axis=0),
                                        in_=XR[:, t, :], in_offset=None).then_inc(scattered, 16)

            def gather(u, t):
                for tab in dict.fromkeys([UNITS[u]["keys"], UNITS[u]["values"]]):
                    g = BATCH_OF[u, t, tab]
                    w = UNITS[u]["w"] * B
                    if g >= NRB:
                        scores_only, j = last_used(g)
                        if scores_only:
                            pool.wait_ge(keys_used, j - NT * (HEADS + 2) + 1)
                        else:
                            pool.wait_ge(summed, j + 1)
                    for k in range(SLOTS[t]):
                        pool.indirect_dma_start(
                            out=rowbuf[g % NRB][:, k * w:(k + 1) * w], out_offset=None,
                            in_=h2_table if tab == H2 else tabs[UNITS[u]["layer"]],
                            element_offset=0 if tab == H2 else tab * N * w,
                            in_offset=bass.IndirectOffsetOnAxis(ap=gidx[:, t, k:k + 1], axis=0)
                        ).then_inc(gathered[g % NRB], 16)

            def put_back(t):
                pool.wait_ge(x_final, t + 1)
                pool.indirect_dma_start(out=finished, out_offset=bass.IndirectOffsetOnAxis(ap=node[:, t, :], axis=0),
                                        in_=X[:, t, :], in_offset=None).then_inc(put_in_order, 16)

            def centre(layer, t):
                if layer < 3 and 0 <= t < NT:
                    n, v = NT * layer + t, slice(B * t, B * (t + 1))
                    pool.wait_ge(mean_made, n + 1)
                    pool.tensor_tensor(bd(H[:, t, :]), bd(X[:, t, :]), over_d(stats[:, 1, v], B), ALU.subtract)\
                        .then_inc(centred, 1)

            def finish(u, i):
                if 1 <= u <= HEADS and 2 <= i <= NT + 1:
                    n = NT * (u - 1) + i - 2
                    z = hT[:, n % 2, :]
                    pool.wait_ge(zT_made, n + 1)
                    pool.tensor_tensor(z, z, aux[:, n % 2, :], ALU.add).then_inc(zT_leaky, 1)
                if 1 <= u <= HEADS and 5 <= i <= NT + 4:
                    t, n = i - 5, NT * (u - 1) + i - 5
                    pool.wait_ge(wo_out, n + 1)
                    if u > 1:
                        if u > 2:
                            pool.wait_ge(h2_summed, n - 2 * NT + 1)
                        pool.tensor_tensor(H[:, t, :], stage[:, n % NST, :], H[:, t, :], ALU.add).then_inc(h2_summed, 1)
                if u == HEADS + 1 and 3 <= i <= NT + 2:
                    t = i - 3
                    o = ot[:, (u * NT + t) % NOT, :]
                    pool.wait_ge(z_inverse, t + 1)
                    pool.tensor_tensor(bd(o), bd(o), over_d(ln[:, 1, (t % 2) * B:(t % 2 + 1) * B], B), ALU.mult)\
                        .then_inc(z_affine, 1)
                    pool.wait_ge(z_affine, 3 * t + 1)
                    pool.tensor_tensor(bd(o), bd(o), feature(1), ALU.mult).then_inc(z_affine, 1)
                    pool.wait_ge(z_affine, 3 * t + 2)
                    pool.tensor_tensor(bd(o), bd(o), feature(2), ALU.add).then_inc(z_affine, 1)
                    pool.wait_ge(z_affine, 3 * t + 3)
                    pool.tensor_tensor(X[:, t, :], o, X[:, t, :], ALU.add).then_inc(x1_made, 1)
                if u == HEADS + 1 and 1 <= i <= NT:
                    t = i - 1
                    o = ot[:, (u * NT + t) % NOT, :]
                    pool.wait_ge(z_mean, t + 1)
                    pool.tensor_tensor(bd(o), bd(o), over_d(ln[:, 0, (t % 2) * B:(t % 2 + 1) * B], B), ALU.subtract)\
                        .then_inc(z_centred, 1)

            for t in range(NT):
                centre(0, t)
            pool.wait_ge(info_loaded, 16)
            pool.wait_ge(flag_made, 1)
            far = pool.value_load(flag[0:1, 0:1], min_val=0, max_val=1)
            with pool.If(far == 0):
                for layer in range(4):
                    for i in range(NST):
                        pool.wait_ge(stage_stored[i], stored_by(layer, i))
                    for group in BRANCHES[layer]:
                        if UNITS[group[0]]["own"] is None:
                            pool.wait_ge(h2_stored, 16 * NT)
                        jobs = [(u, t) for u in group for t in range(NT)]
                        for ut in jobs[:AHEAD]:
                            gather(*ut)
                        for s, step in enumerate(near_steps(group)):
                            for u, i in step:
                                finish(u, i - 2)
                                if u in LAG:
                                    centre(layer + 1, i - 2 - LAG[u])
                            if s + AHEAD < len(jobs):
                                gather(*jobs[s + AHEAD])
            with pool.Else():
                for u in range(len(UNITS)):
                    for i in range(steps(u)):
                        finish(u, i)
                        if u in LAG:
                            centre(UNITS[u]["layer"] + 1, i - LAG[u])
            for t in range(NT):
                put_back(t)

        @block.scalar
        def _(act):
            for i in range(2):
                for q, w in enumerate([L0_W, L2_key, L2_weight, L2_query]):
                    act.dma_start(wload[i * D:(i + 1) * D, q * D:(q + 1) * D], w).then_inc(w_in, 16)
                for hh in range(2):
                    act.dma_start(wload[:, (4 + 2 * hh + i) * D:(5 + 2 * hh + i) * D],
                                  L1_Wh.rearrange("h d c -> (h d) c")[hh * P:(hh + 1) * P, :]).then_inc(w_in, 16)
                act.dma_start(wload[0:D, 8 * D:16 * D].rearrange("p (h i d) -> p h i d", h=HEADS, i=2)[:, :, i, :],
                              L1_Wo.rearrange("o (h d) -> o h d", h=HEADS)).then_inc(w_in, 16)
                act.dma_start(wload[D:P, (8 + i) * D:(9 + i) * D], L3_W).then_inc(w_in, 16)
                act.dma_start(turned[0:HEADS, 2, i * D:(i + 1) * D], L1_bh).then_inc(w_in, 16)
            act.dma_start(turned[0:NT, 0, :], L0_gamma.rearrange("(t p) -> t p", p=P)).then_inc(w_in, 16)
            act.dma_start(turned[0:NT, 1, :], L0_beta.rearrange("(t p) -> t p", p=P)).then_inc(w_in, 16)
            act.dma_start(abc[:, 0, :], L0_a.rearrange("a o -> (a o)").partition_broadcast(P)).then_inc(w_in, 16)
            act.dma_start(abc[:, 1, :], L3_a.rearrange("a o -> (a o)").partition_broadcast(P)).then_inc(w_in, 16)
            for i, v in enumerate([L1_bo, L1_gamma, L1_beta]):
                act.dma_start(rows64[:, i, :], v.partition_broadcast(P)).then_inc(w_in, 16)
            act.wait_ge(key_rows, 16)
            for c in range(ACT_RANKS):
                ins = act.activation(act_junk, brow, ACT.Sign, bias=negkey[:, c:c + 1], accum_out=signs[:, c:c + 1])
                if c < ACT_RANKS - 1:
                    ins.then_inc(sign_made, 1)
                    act.wait_ge(sign_made, c + 1)
            ins.then_inc(signs_summed, 1)
            act.wait_ge(place_rows, 16)
            for t in range(NT):
                act.dma_start(XR[:, t, 0:E].rearrange("p (b d) -> p b d", b=B),
                              x[:, t * P:(t + 1) * P, :].rearrange("b n d -> n b d")).then_inc(x_in, 16)

            def prepare(layer, s):
                if 0 <= s < NT:
                    n = NT * layer + s
                    act.wait_ge(centred, n + 1)
                    if n >= 1:
                        act.wait_ge(var_made, n)
                    act.activation(sq[:, :], H[:, s, :], ACT.Square).then_inc(squared, 1)
                if 0 <= s - 1 < NT:
                    n, v = NT * layer + s - 1, slice(B * (s - 1), B * s)
                    act.wait_ge(var_made, n + 1)
                    act.activation(sd[:, v], stats[:, 2, v], ACT.Sqrt, bias=epsc[:, 0:1], scale=1.0 / D)\
                       .then_inc(sd_made, 1)
                if 0 <= s - 3 < NT:
                    n = NT * layer + s - 3
                    act.wait_ge(h_turned, n + 1)
                    act.activation(hT[:, n % 2, :], tps[n % 2][:, :], ACT.Copy).then_inc(hT_made, 1)
                if 0 <= s - 4 < NT:
                    ng, w = PROJ[layer]
                    for q in range(4):
                        m = 4 * (NT * layer + s - 4) + q
                        act.wait_ge(projected, m + 1)
                        if m >= NST:
                            act.wait_ge(stage_stored[m % NST], 16 * (m // NST))
                        act.activation(stage[:, m % NST, 0:2 * ng * w], proj[q][:, 0:2 * ng * w],
                                       ACT.Copy).then_inc(staged, 1)

            def exp(j):
                act.wait_ge(scored, j + 1)
                w = SLOTS[j % NT] * B
                act.activation(sc[:, j % NSC, 0:w], sc[:, j % NSC, 0:w], ACT.Exp).then_inc(exped, 1)

            def weigh(u, t):
                un, j, K, w = UNITS[u], NT * u + t, SLOTS[t], UNITS[u]["w"]
                g = BATCH_OF[u, t, un["values"]]
                rows = rowbuf[g % NRB][:, 0:K * w * B].rearrange("p (k b c) -> p k b c", k=K, b=B)
                act.wait_ge(normed, j + 1)
                act.wait_ge(gathered[g % NRB], gathered_by(g))
                for k in range(K - act_slots(u, t), K):
                    for b in range(B):
                        v = rows[:, k, b, 0:D]
                        ins = act.activation(v, v, ACT.Copy, scale=sc[:, j % NSC, k * B + b:k * B + b + 1])
                ins.then_inc(act_weighed, 1)

            def take_out(u, t):
                j = NT * u + t
                act.wait_ge(summed, j + 1)
                m = NT * (u - 1) + t
                if u == 0 and t >= NOT:
                    act.wait_ge(centred, NT + t - NOT + 1)
                if u > 0 and m >= NOT:
                    act.wait_ge(z_turned, m - NOT + 1)
                act.activation(ot[:, j % NOT, :], sums[j % 2][:, :], ACT.Copy).then_inc(attended, 1)

            def elu_exp(u, i):
                if u == 0 and 2 <= i <= NT + 1:
                    t = i - 2
                    act.wait_ge(elu_in, t + 1)
                    act.activation(aux[:, t % 2, :], aux[:, t % 2, :], ACT.Exp).then_inc(elu_exped, 1)

            def finish(u, i):
                if u == 0 and 1 <= i <= NT:
                    act.wait_ge(bn_made, i)
                    act.activation(bn[:, (i - 1) % 2, 8:9], bn[:, (i - 1) % 2, 7:8], ACT.Sqrt,
                                   bias=epsc[:, 0:1]).then_inc(bn_rooted, 1)
                if 1 <= u <= HEADS and 1 <= i <= NT:
                    h, n = u - 1, NT * (u - 1) + i - 1
                    act.wait_ge(z_turned, n + 1)
                    if n >= 2:
                        act.wait_ge(wo_made, n - 1)
                    act.activation(hT[:, n % 2, :], tps[n % 2][:, :], ACT.Identity, scale=0.2,
                                   bias=bh[:, h:h + 1])
                    act.activation(aux[:, n % 2, :], tps[n % 2][:, :], ACT.Relu, scale=0.8,
                                   bias=bh[:, HEADS + h:HEADS + h + 1]).then_inc(zT_made, 1)
                if 1 <= u <= HEADS and 4 <= i <= NT + 3:
                    t, n = i - 4, NT * (u - 1) + i - 4
                    act.wait_ge(wo_made, n + 1)
                    if n >= NT + NST:
                        act.wait_ge(h2_summed, n - NT - NST + 1)
                    act.activation(H[:, t, :] if u == 1 else stage[:, n % NST, :], wps[n % 2][:, :],
                                   ACT.Copy).then_inc(wo_out, 1)
                if u == 5 and 1 <= i <= NT:
                    t = i - 1
                    act.wait_ge(z_centred, t + 1)
                    act.activation(aux[:, t % 2, :], ot[:, (5 * NT + t) % NOT, :], ACT.Square).then_inc(z_squared, 1)
                if u == 5 and 2 <= i <= NT + 1:
                    t = i - 2
                    act.wait_ge(z_var, t + 1)
                    act.activation(ln[:, 3, (t % 2) * B:(t % 2 + 1) * B], ln[:, 2, (t % 2) * B:(t % 2 + 1) * B],
                                   ACT.Sqrt, bias=epsc[:, 0:1], scale=1.0 / D).then_inc(z_rooted, 1)

            def attend_far(u):
                kw = 2 if UNITS[u]["add"] else D
                with act.Fori(0, B) as b:
                    act.wait_ge(far_kT_made, B * u + b + 1)
                    with act.Fori(0, NT) as t:
                        n = NT * (B * u + b) + t
                        act.wait_ge(far_scored, n + 1)
                        act.activation(far_q[0:kw, :], far_qT[0:kw, bass.ds(t * P, P)], ACT.Copy).then_inc(far_q_made, 1)
                        act.wait_ge(far_masked, n + 1)
                        act.activation(far_e, far_e, ACT.Exp, bias=far_sum[:, 2:3],
                                       accum_out=far_sum[:, 0:1]).then_inc(far_exped, 1)

            for s in range(NT + PREP - 1):
                prepare(0, s)
            act.wait_ge(flag_made, 1)
            far = act.value_load(flag[0:1, 0:1], min_val=0, max_val=1)
            for layer in range(4):
                with act.If(far == 0):
                    for step in sum(map(list, map(near_steps, BRANCHES[layer])), []):
                        for u, i in step:
                            if 1 <= i <= NT:
                                exp(u * NT + i - 1)
                            elu_exp(u, i - 2)
                            if 1 <= i <= NT:
                                weigh(u, i - 1)
                            if u <= HEADS and 2 <= i <= NT + 1:
                                take_out(u, i - 2)
                            finish(u, i - 2)
                            if u in LAG:
                                prepare(layer + 1, i - 2 - LAG[u])
                with act.Else():
                    for u in sum(BRANCHES[layer], []):
                        attend_far(u)
                        for i in range(steps(u)):
                            elu_exp(u, i)
                            finish(u, i)
                            if u in LAG:
                                prepare(layer + 1, i - LAG[u])

        @block.tensor
        def _(pe):
            pe.wait_ge(ident_made, 3)
            pe.wait_ge(w_in, W_LOADS)
            for hh in range(2):
                pe.transpose(tps[0][:, hh * P:(hh + 1) * P], wload[:, (4 + 2 * hh) * D:(6 + 2 * hh) * D], ident[:, :])
            for h in range(HEADS):
                pe.transpose(tps[1][:, h * D:(h + 1) * D], wload[0:D, (8 + 2 * h) * D:(10 + 2 * h) * D],
                             ident[0:D, 0:D])
            for i in range(2):
                pe.transpose(wps[1][:, i * NT:(i + 1) * NT], turned[0:NT, i, :], ident[0:NT, 0:NT])
            pe.transpose(wps[1][:, 2 * NT:2 * NT + HEADS], turned[0:HEADS, 2, :], ident[0:HEADS, 0:HEADS])
            pe.transpose(tps[0][:, 2 * P:2 * P + D], wload[D:P, 8 * D:10 * D], ident[D:P, D:P]).then_inc(w_turned, 1)
            pe.wait_ge(bad_made, 1)
            pe.matmul(wps[0][:, 0:1], ones[:, :], small[:, 15, 0:1], start=True, stop=True).then_inc(bad_summed, 1)

            def prepare(layer, s):
                if 0 <= s - 2 < NT:
                    n = NT * layer + s - 2
                    pe.wait_ge(h_made, n + 1)
                    if n >= 2:
                        pe.wait_ge(hT_made, n - 1)
                    for q in range(4):
                        mm = pe.transpose(tps[n % 2][:, q * P:(q + 1) * P], H[:, s - 2, q * P:(q + 1) * P], ident[:, :])
                    mm.then_inc(h_turned, 1)
                if 0 <= s - 3 < NT:
                    n = NT * layer + s - 3
                    wb = WB[layer][:, :, :, :].rearrange("p g i c -> p (g i c)")
                    pe.wait_ge(hT_made, n + 1)
                    for q in range(4):
                        m = 4 * n + q
                        if m >= 4:
                            pe.wait_ge(staged, m - 3)
                        pe.matmul(proj[q][:, 0:wb.shape[1]], hT[:, n % 2, q * P:(q + 1) * P], wb,
                                  start=True, stop=True).then_inc(projected, 1)

            def add_up(u, t):
                j, K, w = NT * u + t, SLOTS[t], UNITS[u]["w"]
                g = BATCH_OF[u, t, UNITS[u]["values"]]
                rows = rowbuf[g % NRB][:, 0:K * w * B].rearrange("p (k b c) -> p k b c", k=K, b=B)
                before = j - 2
                if 0 <= before < NT * (HEADS + 1):
                    pe.wait_ge(attended, before + 1)
                elif 0 <= before < NT * (HEADS + 3):
                    pe.wait_ge(sum_used, before - NT * (HEADS + 1) + 1)
                elif before >= 0:
                    pe.wait_ge(x_final, before - NT * (HEADS + 3) + 1)
                pe.wait_ge(weighed, j + 1)
                to = sums[j % 2][:, :].rearrange("p (b d) -> p b d", b=B)
                n = K - act_slots(u, t)
                slots = [*range(n - folded(u, t)), *range(n, K)]
                for k in slots:
                    if k == n:
                        pe.wait_ge(act_weighed, j + 1)
                    mm = pe.matmul(to, ident[:, :], rows[:, k, :, 0:D], start=(k == slots[0]), stop=(k == slots[-1]))
                mm.then_inc(summed, 1)

            def finish(u, i):
                if 1 <= u <= HEADS and 1 <= i <= NT:
                    n = NT * (u - 1) + i - 1
                    pe.wait_ge(attended, NT + n + 1)
                    if n >= 2:
                        pe.wait_ge(zT_made, n - 1)
                    for q in range(4):
                        mm = pe.transpose(tps[n % 2][:, q * P:(q + 1) * P],
                                          ot[:, (NT + n) % NOT, q * P:(q + 1) * P], ident[:, :])
                    mm.then_inc(z_turned, 1)
                if 1 <= u <= HEADS and 3 <= i <= NT + 2:
                    n = NT * (u - 1) + i - 3
                    pe.wait_ge(zT_leaky, n + 1)
                    if n >= 2:
                        pe.wait_ge(wo_out, n - 1)
                    for q in range(4):
                        mm = pe.matmul(wps[n % 2][:, q * P:(q + 1) * P], hT[:, n % 2, q * P:(q + 1) * P],
                                       WoB[:, u - 1, :, :].rearrange("p i c -> p (i c)"),
                                       start=True, stop=True)
                    mm.then_inc(wo_made, 1)

            def attend_far(u):
                un = UNITS[u]
                w, kw = un["w"], 2 if un["add"] else D
                keys, values, queries = (r[:, 0:NT * w].rearrange("p (t c) -> p t c", t=NT) for r in far_rows)
                if un["add"]:
                    keys, queries = far_pairs
                if 2 <= u <= HEADS + 1:
                    pe.wait_ge(wo_out, NT * (u - 1))
                with pe.Fori(0, B) as b:
                    pe.wait_ge(far_source, B * u + b + 1)
                    for c in range(NT):
                        pe.matmul(pps[c // 4][0:kw, (c % 4) * P:(c % 4 + 1) * P], keys[:, c, 0:kw], ident[:, :],
                                  start=True, stop=True)
                        mm = pe.matmul((tps + wps)[c // 4][0:kw, (c % 4) * P:(c % 4 + 1) * P],
                                       queries[:, c, 0:kw], ident[:, :], start=True, stop=True)
                    mm.then_inc(far_turned, 1)
                    with pe.Fori(0, NT) as t:
                        n = NT * (B * u + b) + t
                        pe.wait_ge(far_q_made, n + 1)
                        for q in range(4):
                            mm = pe.matmul(pps[q][:, :], far_q[0:kw, :], far_kT[0:kw, q * 512:(q + 1) * 512],
                                           start=True, stop=True)
                        mm.then_inc(far_scored, 1)
                        pe.wait_ge(far_exped, n + 1)
                        for c in range(NT):
                            mm = pe.transpose(pps[c // 4][:, (c % 4) * P:(c % 4 + 1) * P],
                                              far_e[:, c * P:(c + 1) * P], ident[:, :])
                        mm.then_inc(far_p_turned, 1)
                        pe.wait_ge(far_pT_made, n + 1)
                        for c in range(NT):
                            mm = pe.matmul(tps[0][:, 0:D], far_pT[:, c * P:(c + 1) * P], values[:, c, 0:D],
                                           start=(c == 0), stop=(c == NT - 1))
                        mm.then_inc(far_summed, 1)

            pe.wait_ge(w_built, 1)
            for i in range(NT + PREP - 1):
                prepare(0, i)
            pe.wait_ge(flag_made, 1)
            far = pe.value_load(flag[0:1, 0:1], min_val=0, max_val=1)
            for layer in range(4):
                with pe.If(far == 0):
                    for step in sum(map(list, map(near_steps, BRANCHES[layer])), []):
                        for u, i in step:
                            finish(u, i - 2)
                            if u in LAG:
                                prepare(layer + 1, i - 2 - LAG[u])
                        for u, i in step:
                            if 1 <= i <= NT:
                                add_up(u, i - 1)
                with pe.Else():
                    for u in sum(BRANCHES[layer], []):
                        attend_far(u)
                        for i in range(steps(u)):
                            finish(u, i)
                            if u in LAG:
                                prepare(layer + 1, i - LAG[u])

        @block.vector
        def _(dve):
            part = ["order", 0]

            def run(ins):
                part[1] += 1
                ins.then_inc(dve_done[part[0]], 1)
                dve.wait_ge(dve_done[part[0]], part[1])

            def tell(ins, to, value):
                ins.then_inc(to, 1)
                dve.wait_ge(to, value)

            deg, key, rank, place1, place = (small[:, i, :] for i in (0, 2, 3, 4, 1))
            diag, nvalid, nodef, cap = small[:, 5, :], small[:, 6, :], small[:, 7, :], small[:, 8, :]
            tmp, bad, tmp2 = small[:, 9, :], small[:, 10, :], small[:, 11, :]
            allbad, badflag = small[:, 15, 0:1], small[:, 14, 0:1]

            run(dve.memset(epsc[:, :], EPS))
            for s in (far_summed, far_bias_made, far_scored):
                tell(dve.memset(far_sum[:, :], 0.0), s, 1)
            dve.wait_ge(ident_made, 3)
            for c in range(NT):
                dve.wait_ge(adj_loaded[c % 3], 16 * (c // 3 + 1))
                tell(dve.tensor_scalar(mask[:, c, :], adjt[:, c % 3, :], 0.0, None, ALU.is_gt, ALU.add,
                                       accum_out=deg[:, c:c + 1]), adj_used, c + 1)
                run(dve.tensor_tensor_reduce(junk[:, 0:P], mask[:, c, c * P:(c + 1) * P], ident[:, :], 1.0, 0.0,
                                             ALU.mult, ALU.add, diag[:, c:c + 1]))
            dve.wait_ge(iota_made, 1)
            run(dve.tensor_copy(nodef, iot[:, :]))
            run(dve.tensor_scalar(tmp, nodef, -1.0, float(N - 1), ALU.mult, ALU.add))
            run(dve.scalar_tensor_tensor(key, deg, float(N), tmp, ALU.mult, ALU.add))
            tell(dve.tensor_scalar(negkey, key, -1.0, None, ALU.mult), key_made, 1)
            for w in (*WB, WoB):
                run(dve.memset(w[:, :, :, :], 0.0))
            dve.wait_ge(w_in, W_LOADS)
            dve.wait_ge(w_turned, 1)
            run(dve.tensor_copy(XR[:, :, E:E + 2].rearrange("p t i -> p i t"),
                                wps[1][:, 0:2 * NT].rearrange("p (i t) -> p i t", i=2)))
            for i, f in enumerate((0.2, 0.8)):
                run(dve.tensor_scalar(bh[:, i * HEADS:(i + 1) * HEADS], wps[1][:, 2 * NT:2 * NT + HEADS], f, None,
                                      ALU.mult))
            for i in range(2):
                lo, hi = i * D, (i + 1) * D
                run(dve.tensor_copy(WB[0][lo:hi, 0, i, 0:D], wload[lo:hi, 0:D]))
                run(dve.tensor_copy(WB[2][lo:hi, :, i, :], wload[lo:hi, D:4 * D].rearrange("p (g d) -> p g d", g=3)))
                run(dve.tensor_copy(WB[1][lo:hi, :, i, :], tps[0][lo:hi, 0:2 * P].rearrange("p (g d) -> p g d", g=HEADS)))
                run(dve.tensor_copy(WoB[lo:hi, :, i, :], tps[1][lo:hi, 0:2 * P].rearrange("p (g d) -> p g d", g=HEADS)))
                run(dve.tensor_copy(WB[3][lo:hi, 0, i, 0:D], tps[0][lo:hi, 2 * P:2 * P + D]))
                for l, wb in enumerate((WB[0], WB[3])):
                    for c, half in ((D, 1), (D + 1, 0)):
                        run(dve.tensor_tensor(wtmp[lo:hi, :], wb[lo:hi, 0, i, 0:D],
                                              abc[lo:hi, l, half * D:(half + 1) * D], ALU.mult))
                        run(dve.tensor_reduce(wb[lo:hi, 0, i, c:c + 1], wtmp[lo:hi, :], AX.X, ALU.add))
            tell(dve.memset(tmp, 0.0), w_built, 1)
            dve.wait_ge(key_rows, 16)
            for c in range(ACT_RANKS, NT):
                run(dve.tensor_scalar(junk, brow, key[:, c:c + 1], None, ALU.is_gt, ALU.add,
                                      accum_out=rank[:, c:c + 1]))
            dve.wait_ge(signs_summed, 1)
            run(dve.tensor_scalar(rank[:, 0:ACT_RANKS], signs[:, 0:ACT_RANKS], 0.5, (N - 1) / 2,
                                  ALU.mult, ALU.add))
            run(dve.tensor_scalar(place, rank, float(P * PLACE_OF[0]), None, ALU.add))
            for r in range(1, NT):
                further = PLACE_OF[r] - PLACE_OF[r - 1] - 1
                if further:
                    run(dve.tensor_scalar(tmp, rank, float(P * r), float(P * further), ALU.is_ge, ALU.mult))
                    run(dve.tensor_tensor(place, place, tmp, ALU.add))
            tell(dve.tensor_scalar(place1, place, 1.0, None, ALU.add), place_made, 1)
            run(dve.memset(cap, float(BY_RANK[-1])))
            for t in range(NT - 1):
                if BY_RANK[t] > BY_RANK[t + 1]:
                    run(dve.tensor_scalar(tmp, rank, float(P * (t + 1)), float(BY_RANK[t] - BY_RANK[t + 1]),
                                          ALU.is_lt, ALU.mult))
                    run(dve.tensor_tensor(cap, cap, tmp, ALU.add))
            dve.wait_ge(place_rows, 16)
            tell(dve.tensor_copy(places.rearrange("p (t q) -> p t q", t=NT),
                                 brow.rearrange("p (q t) -> p t q", t=NT)), places_made, 1)
            for c in range(NT):
                if c in POOL_RANKED:
                    i = POOL_RANKED.index(c)
                    ranked = pool_ranked[i % 3]
                    dve.wait_ge(ranked_made, i + 1)
                else:
                    ranked = dve_ranked
                    run(dve.tensor_tensor(ranked, mask[:, c, :], places, ALU.mult))
                for q in range(4):
                    ins = dve.max(cand[:, 0, q * 8:(q + 1) * 8], ranked[:, q * (N // 4):(q + 1) * (N // 4)])
                    if c in POOL_RANKED and q == 3:
                        tell(ins, ranked_used, i + 1)
                    else:
                        run(ins)
                run(dve.max(lists[:, c, 0:8], cand[:, 0, :]))
                run(dve.match_replace(cand[:, 1, :], lists[:, c, 0:8], cand[:, 0, :], 0.0))
                run(dve.max(lists[:, c, 8:16], cand[:, 1, :]))
            run(dve.tensor_scalar(valid[:, :, :], lists[:, :, :], 0.0, None, ALU.is_gt))
            run(dve.tensor_reduce(nvalid, valid[:, :, :], AX.X, ALU.add))
            run(dve.tensor_scalar(lists[:, :, :], lists[:, :, :], -1.0, 0.0, ALU.add, ALU.max))
            run(dve.tensor_copy(XR[:, :, E + 2:E + 2 + NL].bitcast(I32), lists[:, :, :]))
            run(dve.tensor_scalar(XR[:, :, E + 2 + NL:E + 2 + 2 * NL], valid[:, :, :], -NEG, NEG, ALU.mult, ALU.add))
            run(dve.tensor_copy(XR[:, :, XS - 1].bitcast(I32), iot[:, :]))
            run(dve.tensor_tensor(bad, deg, cap, ALU.is_gt))
            run(dve.tensor_scalar(tmp, diag, 1.0, None, ALU.is_lt))
            run(dve.tensor_tensor(bad, bad, tmp, ALU.add))
            run(dve.tensor_tensor(tmp, nvalid, deg, ALU.not_equal))
            run(dve.tensor_tensor(bad, bad, tmp, ALU.add))
            tell(dve.tensor_reduce(allbad, bad, AX.X, ALU.add), bad_made, 1)
            dve.wait_ge(bad_summed, 1)
            run(dve.tensor_scalar(badflag, wps[0][:, 0:1], 0.0, None, ALU.is_gt))
            tell(dve.tensor_copy(flag[:, :], badflag), flag_made, 1)
            run(dve.tensor_tensor(tmp, nodef, place, ALU.subtract))
            run(dve.scalar_tensor_tensor(tmp2, tmp, badflag, place, ALU.mult, ALU.add))
            tell(dve.tensor_copy(placei[:, :], tmp2), ordered, 1)
            dve.wait_ge(info_loaded, 16)

            def prepare(layer, s):
                if 0 <= s < NT:
                    n, v = NT * layer + s, slice(B * s, B * (s + 1))
                    if layer == 0 and s % 4 == 0:
                        dve.wait_ge(x_loaded[s // 4], 16)
                    if layer == 2:
                        dve.wait_ge(x1_made, s + 1)
                    run(dve.tensor_reduce(stats[:, 0, v], bd(X[:, s, :]), AX.X, ALU.add))
                    ins = dve.tensor_scalar(stats[:, 1, v], stats[:, 0, v], 1.0 / D, None, ALU.mult)
                    if layer < 3:
                        tell(ins, mean_made, n + 1)
                    else:
                        run(ins)
                        tell(dve.tensor_tensor(bd(H[:, s, :]), bd(X[:, s, :]), over_d(stats[:, 1, v], B),
                                               ALU.subtract), centred, n + 1)
                if 0 <= s - 1 < NT:
                    n, v = NT * layer + s - 1, slice(B * (s - 1), B * s)
                    dve.wait_ge(squared, n + 1)
                    tell(dve.tensor_reduce(stats[:, 2, v], bd(sq[:, :]), AX.X, ALU.add), var_made, n + 1)
                if 0 <= s - 2 < NT:
                    t, n, v = s - 2, NT * layer + s - 2, slice(B * (s - 2), B * (s - 1))
                    dve.wait_ge(sd_made, n + 1)
                    run(dve.reciprocal(stats[:, 3, v], sd[:, v]))
                    tell(dve.scalar_tensor_tensor(bd(H[:, t, :]), bd(H[:, t, :]), 0.0, over_d(stats[:, 3, v], B),
                                                  ALU.max, ALU.mult), h_made, n + 1)

            def score(u, t):
                un, j, K = UNITS[u], NT * u + t, SLOTS[t]
                g = BATCH_OF[u, t, un["keys"]]
                w = un["w"]
                S = sc[:, j % NSC, 0:K * B].rearrange("p (k b) -> p k b", k=K)
                S2 = sc2[:, 0:K * B].rearrange("p (k b) -> p k b", k=K)
                if j >= NSC:
                    dve.wait_ge(act_weighed, j - NSC + 1)
                dve.wait_ge(gathered[g % NRB], gathered_by(g))
                if un["own"] is not None:
                    o = OWN_OF[u, t]
                    dve.wait_ge(own_loaded[o % NOWN], 16 * (o // NOWN + 1))
                    mine = own[:, o % NOWN, 0:w * B]
                else:
                    mine = H[:, t, :]
                rows = rowbuf[g % NRB][:, 0:K * w * B]
                if un["add"]:
                    source = rows.rearrange("p (k b c) -> p k b c", k=K, b=B)[:, :, :, D]
                    self_ = mine.rearrange("p (b c) -> p b c", b=B)[:, :, D + 1].unsqueeze(1).to_broadcast([P, K, B])
                    tell(dve.tensor_tensor(S, source, self_, ALU.add), own_used, o + 1)
                else:
                    chunks = -(-K // CHUNK)
                    for c in range(chunks):
                        k = K * c // chunks
                        n = K * (c + 1) // chunks - k
                        pr = prod[:, 0:n * E]
                        last = k + n == K and un["own"] is not None
                        ins = dve.tensor_tensor(pr.rearrange("p (k e) -> p k e", k=n),
                                                rows.rearrange("p (k e) -> p k e", k=K)[:, k:k + n, :],
                                                mine.unsqueeze(1).to_broadcast([P, n, E]), ALU.mult)
                        if last:
                            tell(ins, own_used, o + 1)
                        else:
                            run(ins)
                        ins = dve.tensor_reduce(sc[:, j % NSC, k * B:(k + n) * B], bd(pr), AX.X, ALU.add)
                        if k + n == K and un["keys"] != un["values"]:
                            tell(ins, keys_used, t + 1)
                        else:
                            run(ins)
                if un["slope"] is not None:
                    run(dve.scalar_tensor_tensor(S2, S, un["slope"], S, ALU.mult, ALU.max))
                else:
                    S2 = S
                mb = gbias[:, t, 0:K].unsqueeze(2).to_broadcast([P, K, B])
                run(dve.scalar_tensor_tensor(S, S2, un["factor"], mb, ALU.mult, ALU.add))
                run(dve.tensor_reduce(mx[:, 0, :], S.rearrange("p k b -> p b k"), AX.X, ALU.max))
                tell(dve.tensor_tensor(S, S, mx[:, 0, :].unsqueeze(1).to_broadcast([P, K, B]), ALU.subtract),
                     scored, j + 1)

            def attend(u, t):
                un, j, K, w = UNITS[u], NT * u + t, SLOTS[t], UNITS[u]["w"]
                g = BATCH_OF[u, t, un["values"]]
                S = sc[:, j % NSC, 0:K * B].rearrange("p (k b) -> p k b", k=K)
                dve.wait_ge(exped, j + 1)
                run(dve.tensor_reduce(mx[:, 1, :], S.rearrange("p k b -> p b k"), AX.X, ALU.add))
                run(dve.reciprocal(mx[:, 1, :], mx[:, 1, :]))
                tell(dve.tensor_tensor(S, S, mx[:, 1, :].unsqueeze(1).to_broadcast([P, K, B]), ALU.mult),
                     normed, j + 1)
                if un["keys"] != un["values"]:
                    dve.wait_ge(gathered[g % NRB], gathered_by(g))
                n = K - act_slots(u, t)
                v = rowbuf[g % NRB][:, 0:n * w * B].rearrange("p (k b c) -> p k b c", k=n, b=B)[:, :, :, 0:D]
                ins = dve.tensor_tensor(v, v, S[:, 0:n, :].unsqueeze(3).to_broadcast([P, n, B, D]), ALU.mult)
                f = folded(u, t)
                if f:
                    run(ins)
                    ins = dve.tensor_tensor(v[:, 0:f], v[:, 0:f], v[:, n - f:n], ALU.add)
                tell(ins, weighed, j + 1)

            near = [True]

            def output(u, t):
                j = NT * u + t
                if u <= HEADS:
                    dve.wait_ge(attended, j + 1)
                elif near[0]:
                    dve.wait_ge(summed, j + 1)
                    return sums[j % 2][:, :]
                return ot[:, j % NOT, :]

            def finish0(i):
                if 1 <= i <= NT:
                    t = i - 1
                    o, b = output(0, t), bn[:, t % 2, :]
                    run(dve.bn_stats(b[:, 0:6], o))
                    tell(dve.bn_aggr(b[:, 6:8], b[:, 0:6]), bn_made, t + 1)
                if 2 <= i <= NT + 1:
                    t = i - 2
                    o, b, a = ot[:, t % NOT, :], bn[:, t % 2, :], aux[:, t % 2, :]
                    dve.wait_ge(bn_rooted, t + 1)
                    run(dve.reciprocal(b[:, 9:10], b[:, 8:9]))
                    run(dve.tensor_tensor(b[:, 10:11], b[:, 9:10], gamma[:, t, :], ALU.mult))
                    run(dve.scalar_tensor_tensor(o, o, b[:, 6:7], b[:, 10:11].to_broadcast([P, E]), ALU.subtract, ALU.mult))
                    run(dve.scalar_tensor_tensor(o, o, beta[:, t, :], H[:, t, :], ALU.add, ALU.add))
                    tell(dve.tensor_scalar(a, o, 0.0, None, ALU.min), elu_in, t + 1)
                if 3 <= i <= NT + 2:
                    t = i - 3
                    o, a = ot[:, t % NOT, :], aux[:, t % 2, :]
                    dve.wait_ge(elu_exped, t + 1)
                    run(dve.scalar_tensor_tensor(o, o, 0.0, a, ALU.max, ALU.add))
                    run(dve.scalar_tensor_tensor(X[:, t, :], o, -1.0, X[:, t, :], ALU.add, ALU.add))

            def finish1(i):
                if 1 <= i <= NT:
                    t = i - 1
                    o = ot[:, (5 * NT + t) % NOT, :]
                    m = ln[:, 0, (t % 2) * B:(t % 2 + 1) * B]
                    if t >= NOT:
                        dve.wait_ge(x1_made, t - NOT + 1)
                    tell(dve.tensor_tensor(bd(o), bd(output(HEADS + 1, t)), feature(0), ALU.add), sum_used, t + 1)
                    run(dve.scalar_tensor_tensor(o, o, 0.2, o, ALU.mult, ALU.max))
                    run(dve.tensor_reduce(m, bd(o), AX.X, ALU.add))
                    tell(dve.tensor_scalar(m, m, 1.0 / D, None, ALU.mult), z_mean, t + 1)
                if 2 <= i <= NT + 1:
                    t = i - 2
                    dve.wait_ge(z_squared, t + 1)
                    tell(dve.tensor_reduce(ln[:, 2, (t % 2) * B:(t % 2 + 1) * B], bd(aux[:, t % 2, :]), AX.X, ALU.add),
                         z_var, t + 1)
                if 3 <= i <= NT + 2:
                    t = i - 3
                    dve.wait_ge(z_rooted, t + 1)
                    tell(dve.reciprocal(ln[:, 1, (t % 2) * B:(t % 2 + 1) * B], ln[:, 3, (t % 2) * B:(t % 2 + 1) * B]),
                         z_inverse, t + 1)

            def finish(u, i):
                if u == 0:
                    finish0(i)
                elif u == HEADS + 1:
                    finish1(i)
                elif u > HEADS and 1 <= i <= NT:
                    t = i - 1
                    o = output(u, t)
                    if u == HEADS + 2:
                        tell(dve.tensor_tensor(X[:, t, :], o, X[:, t, :], ALU.add), sum_used, NT + t + 1)
                    else:
                        tell(dve.scalar_tensor_tensor(X[:, t, :], o, 0.0, X[:, t, :], ALU.max, ALU.add), x_final, t + 1)

            def attend_near(group):
                if group[0] == HEADS + 1:
                    dve.wait_ge(h2_summed, (HEADS - 1) * NT)
                for step in near_steps(group):
                    for u, i in step:
                        finish(u, i - 2)
                        if u in LAG:
                            prepare(UNITS[u]["layer"] + 1, i - 2 - LAG[u])
                    for u, i in step:
                        if 1 <= i <= NT:
                            attend(u, i - 1)
                    for u, i in step:
                        if i < NT:
                            score(u, i)

            def attend_far(u):
                un = UNITS[u]
                w, kw = un["w"], 2 if un["add"] else D
                keys, queries = (far_rows[i][:, 0:NT * w].rearrange("p (t c) -> p t c", t=NT) for i in (0, 2))
                ops_b = 7 + 4 * un["add"]
                ops_t = 11 + (un["slope"] is not None) + (un["layer"] in (1, 2))
                done = dve_done_far[u]
                with dve.Fori(0, B) as b:
                    m = B * u + b
                    at = [0]

                    def chain(ins, before):
                        at[0] += 1
                        ins.then_inc(done, 1)
                        dve.wait_ge(done, before + at[0])

                    before = b * (ops_b + NT * ops_t)
                    dve.wait_ge(far_loaded, 48 * (m + 1))
                    if un["add"]:
                        chain(dve.memset(far_pairs[0], 1.0), before)
                        chain(dve.memset(far_pairs[1], 1.0), before)
                        chain(dve.tensor_copy(far_pairs[0][:, :, 0], keys[:, :, D]), before)
                        chain(dve.tensor_copy(far_pairs[1][:, :, 1], queries[:, :, D + 1]), before)
                    dve.memset(far_sum[:, 1:2], 0.0).then_inc(far_source, 1)
                    dve.wait_ge(far_turned, m + 1)
                    for q in range(4):
                        chain(dve.tensor_copy(far_kT[0:kw, q * 512:(q + 1) * 512], pps[q][0:kw, :]), before)
                    for q in range(4):
                        ins = dve.tensor_copy(far_qT[0:kw, q * 512:(q + 1) * 512], (tps + wps)[q][0:kw, :])
                        if q < 3:
                            chain(ins, before)
                    ins.then_inc(far_kT_made, 1)
                    assert at[0] == ops_b
                    with dve.Fori(0, NT) as t:
                        n = NT * m + t
                        at[0] = 0
                        before = b * (ops_b + NT * ops_t) + ops_b + t * ops_t
                        dve.wait_ge(far_adj_loaded, 16 * (n + 1))
                        dve.tensor_scalar(far_bias, far_adj, 0.0, NEG, ALU.is_le, ALU.mult).then_inc(far_bias_made, 1)
                        dve.wait_ge(far_bias_made, n + 2)
                        if un["layer"] in (1, 2):
                            block_ = far_bias[:, bass.ds(t * P, P)]
                            chain(dve.scalar_tensor_tensor(block_, other, 1.0, block_, ALU.mult, ALU.mult), before)
                        dve.wait_ge(far_scored, n + 2)
                        for q in range(4):
                            chain(dve.tensor_copy(far_e[:, q * 512:(q + 1) * 512], pps[q][:, :]), before)
                        if un["slope"] is not None:
                            chain(dve.scalar_tensor_tensor(far_e, far_e, un["slope"], far_e, ALU.mult, ALU.max), before)
                        chain(dve.scalar_tensor_tensor(far_e, far_e, un["factor"], far_bias, ALU.mult, ALU.add), before)
                        chain(dve.tensor_reduce(far_sum[:, 1:2], far_e, AX.X, ALU.max), before)
                        dve.tensor_scalar(far_sum[:, 2:3], far_sum[:, 1:2], -1.0, None, ALU.mult).then_inc(far_masked, 1)
                        dve.wait_ge(far_p_turned, n + 1)
                        for q in range(4):
                            ins = dve.tensor_copy(far_pT[:, q * 512:(q + 1) * 512], pps[q][:, :])
                            if q < 3:
                                chain(ins, before)
                        ins.then_inc(far_pT_made, 1)
                        dve.wait_ge(far_summed, n + 2)
                        chain(dve.reciprocal(far_sum[:, 1:2], far_sum[:, 0:1]), before)
                        to = far_out[:, bass.ds(t, 1), bass.ds(b * D, D)].rearrange("p o d -> p (o d)")
                        chain(dve.tensor_scalar(to, tps[0][:, 0:D], far_sum[:, 1:2], None, ALU.mult), before)
                        assert at[0] == ops_t

            def finish_far(u):
                for i in range(steps(u)):
                    if 1 <= i <= NT:
                        m = NT * (u - 1) + i - 1
                        if 1 <= u <= HEADS and m >= NOT:
                            dve.wait_ge(z_turned, m - NOT + 1)
                        if u == HEADS + 1 and i > NOT:
                            dve.wait_ge(x1_made, i - NOT)
                        ins = dve.tensor_copy(ot[:, (NT * u + i - 1) % NOT, :], far_out[:, i - 1, :])
                        if u <= HEADS:
                            tell(ins, attended, NT * u + i)
                        else:
                            run(ins)
                    finish(u, i)
                    if u in LAG:
                        prepare(UNITS[u]["layer"] + 1, i - LAG[u])

            part[:] = ["prep", 0]
            for i in range(NT + PREP - 1):
                prepare(0, i)
            far = dve.value_load(flag[0:1, 0:1], min_val=0, max_val=1)
            for layer in range(4):
                with dve.If(far == 0):
                    part[:] = [f"near{layer}", 0]
                    near[0] = True
                    for group in BRANCHES[layer]:
                        attend_near(group)
                with dve.Else():
                    part[:] = [f"end{layer}", 0]
                    near[0] = False
                    run(dve.tensor_scalar(other, ident[:, :], -1.0, 1.0, ALU.mult, ALU.add))
                    for u in sum(BRANCHES[layer], []):
                        attend_far(u)
                        finish_far(u)


W_LOADS = 16 * (2 * (4 + 2 + 3) + 2 + 2 + 3)

_INS = ['x', 'adj', 'L0_gnn_W', 'L0_gnn_a', 'L0_gnn_gamma', 'L0_gnn_beta', 'L1_gnn_Wh', 'L1_gnn_bh', 'L1_gnn_Wo',
        'L1_gnn_bo', 'L1_gnn_gamma', 'L1_gnn_beta', 'L2_gnn_weight', 'L2_gnn_query', 'L2_gnn_key_p', 'L3_gnn_W',
        'L3_gnn_a']


def kernel(**inputs):
    import numpy as _np
    import concourse.bacc as _bacc
    from concourse import mybir as _mybir
    from concourse.bass_utils import run_bass_kernel_spmd as _run

    nc = _bacc.Bacc("TRN2", target_bir_lowering=False, num_devices=1)
    arrays, args = {}, []
    for name in _INS:
        a = _np.ascontiguousarray(inputs[name])
        arrays[f"in_{name}"] = a
        args.append(nc.dram_tensor(f"in_{name}", a.shape, _mybir.dt.from_np(a.dtype), kind="ExternalInput").ap())
    args.append(nc.dram_tensor("out_0", (B, N, D), _mybir.dt.float32, kind="ExternalOutput").ap())
    program(nc, *args)
    r = _run(nc, [arrays], core_ids=[0])
    return r.results[0]["out_0"]
```
